# Optimizing a Trainium2 kernel written in Bass

```python
import numpy as np
import jax
import jax.numpy as jnp

def _softmax(x, axis=-1):
    return jax.nn.softmax(x, axis=axis)

def _gelu(x):
    return jax.nn.gelu(x, approximate=True)

def _silu(x):
    return jax.nn.silu(x)

def _sigmoid(x):
    return jax.nn.sigmoid(x)

def _layernorm(x, axis=-1, eps=1e-05):
    m = jnp.mean(x, axis=axis, keepdims=True)
    v = jnp.var(x, axis=axis, keepdims=True)
    return (x - m) / jnp.sqrt(v + eps)

def _scatter_add(tgt, idx, src, axis=0):
    return tgt.at[idx].add(src)

def _segment_sum(src, seg, n):
    return jax.ops.segment_sum(src, seg, n)
kernel_name = 'mk_hybrid_d1_jaxref_r8_706085'

def setup_inputs(seed: int=0):
    np.random.seed(seed)
    _w = jnp.asarray

    def _L0_attn_a_setup():
        import jax, jax.numpy as jnp
        import numpy as np
        N_LAYERS = 2
        D_MODEL = 128
        D_STATE = 16
        D_CONV = 4
        EXPAND = 2
        D_INNER = EXPAND * D_MODEL
        DT_RANK = (D_MODEL + 15) // 16
        B, T = (2, 128)
        LN_EPS = 1e-05

        def _layer_norm(x, w, b):
            mu = jnp.mean(x, axis=-1, keepdims=True)
            xc = x - mu
            var = jnp.mean(xc * xc, axis=-1, keepdims=True)
            return xc * jax.lax.rsqrt(var + LN_EPS) * w + b

        def _mamba_layer(x, in_w, cw, cb, xp_w, dt_w, dt_b, A_log, Dskip, out_w):
            xz = jnp.einsum('btd,ed->bte', x, in_w)
            xc, z = jnp.split(xz, 2, axis=-1)
            pad = D_CONV - 1
            xpad = jnp.pad(xc, ((0, 0), (pad, 0), (0, 0)))
            Tlen = xc.shape[1]
            conv = sum((xpad[:, k:k + Tlen, :] * cw[:, k] for k in range(D_CONV))) + cb
            u = jax.nn.silu(conv)
            x_dbl = jnp.einsum('btd,ed->bte', u, xp_w)
            dt, Bm, Cm = jnp.split(x_dbl, [DT_RANK, DT_RANK + D_STATE], axis=-1)
            dt = jax.nn.softplus(jnp.einsum('btr,dr->btd', dt, dt_w) + dt_b)
            A = -jnp.exp(A_log)

            def step(h, inp):
                dt_t, B_t, C_t, u_t = inp
                dA = jnp.exp(dt_t[:, :, None] * A)
                h = dA * h + (dt_t * u_t)[:, :, None] * B_t[:, None, :]
                y = jnp.einsum('bdn,bn->bd', h, C_t)
                return (h, y)
            h0 = jnp.zeros((x.shape[0], D_INNER, D_STATE), x.dtype)
            _, ys = jax.lax.scan(step, h0, (dt.transpose(1, 0, 2), Bm.transpose(1, 0, 2), Cm.transpose(1, 0, 2), u.transpose(1, 0, 2)))
            y = ys.transpose(1, 0, 2) + u * Dskip
            y = y * jax.nn.silu(z)
            return jnp.einsum('bti,oi->bto', y, out_w)
        key = jax.random.key(seed)
        ks = jax.random.split(key, 12)
        L = N_LAYERS
        x = jax.random.normal(ks[0], (B, T, D_MODEL), jnp.float32)
        in_proj_w = 0.02 * jax.random.normal(ks[1], (L, 2 * D_INNER, D_MODEL), jnp.float32)
        conv_w = 0.2 * jax.random.normal(ks[2], (L, D_INNER, D_CONV), jnp.float32)
        conv_b = jnp.zeros((L, D_INNER), jnp.float32)
        x_proj_w = 0.02 * jax.random.normal(ks[3], (L, DT_RANK + 2 * D_STATE, D_INNER), jnp.float32)
        dt_proj_w = 0.02 * jax.random.normal(ks[4], (L, D_INNER, DT_RANK), jnp.float32)
        dt_proj_b = jnp.full((L, D_INNER), -4.6, jnp.float32)
        A_log = jnp.broadcast_to(jnp.log(jnp.arange(1, D_STATE + 1, dtype=jnp.float32)), (L, D_INNER, D_STATE))
        Dskip = jnp.ones((L, D_INNER), jnp.float32)
        out_proj_w = 0.02 * jax.random.normal(ks[5], (L, D_MODEL, D_INNER), jnp.float32)
        ln_w = jnp.ones((L, D_MODEL), jnp.float32)
        ln_b = jnp.zeros((L, D_MODEL), jnp.float32)
        return {'x': x, 'in_proj_w': in_proj_w, 'conv_w': conv_w, 'conv_b': conv_b, 'x_proj_w': x_proj_w, 'dt_proj_w': dt_proj_w, 'dt_proj_b': dt_proj_b, 'A_log': A_log, 'Dskip': Dskip, 'out_proj_w': out_proj_w, 'ln_w': ln_w, 'ln_b': ln_b}
    _L0_attn_a_in = _L0_attn_a_setup()

    def _L0_attn_b_setup():
        import jax, jax.numpy as jnp
        import numpy as np
        B, S, E, H = (2, 256, 128, 16)
        D = E // H
        NEG_INF = -1e+30

        def alibi_slopes(n_head):
            return jnp.asarray([2.0 ** (-8.0 * (i + 1) / n_head) for i in range(n_head)], dtype=jnp.float32)
        key = jax.random.key(seed)
        ks = jax.random.split(key, 5)
        scale = 0.02
        return {'x': jax.random.normal(ks[0], (B, S, E), dtype=jnp.float32), 'W_kqv': jax.random.normal(ks[1], (E, 3 * E), dtype=jnp.float32) * scale, 'b_kqv': jnp.zeros((3 * E,), dtype=jnp.float32), 'W_proj': jax.random.normal(ks[2], (E, E), dtype=jnp.float32) * scale, 'b_proj': jnp.zeros((E,), dtype=jnp.float32), 'slopes': alibi_slopes(H)}
    _L0_attn_b_in = _L0_attn_b_setup()

    def _L0_ffn_setup():
        import jax, jax.numpy as jnp
        import numpy as np
        D, F, E, K = (128, 344, 8, 2)
        key = jax.random.key(seed)
        k0, k1, k2, k3, k4 = jax.random.split(key, 5)
        s = 0.02
        x = jax.random.normal(k0, (2, 64, D), jnp.float32)
        Ws = jax.random.normal(k1, (D, E), jnp.float32) * s
        bs = jnp.zeros((E,), jnp.float32)
        Wg = jax.random.normal(k2, (E, D, F), jnp.float32) * s
        Wu = jax.random.normal(k3, (E, D, F), jnp.float32) * s
        Wd = jax.random.normal(k4, (E, F, D), jnp.float32) * s
        return {'x': x, 'Ws': Ws, 'bs': bs, 'Wg': Wg, 'Wu': Wu, 'Wd': Wd}
    _L0_ffn_in = _L0_ffn_setup()
    _d = {'L0_attn_a_x': _L0_attn_a_in['x'], 'L0_attn_a_in_proj_w': _L0_attn_a_in['in_proj_w'], 'L0_attn_a_conv_w': _L0_attn_a_in['conv_w'], 'L0_attn_a_conv_b': _L0_attn_a_in['conv_b'], 'L0_attn_a_x_proj_w': _L0_attn_a_in['x_proj_w'], 'L0_attn_a_dt_proj_w': _L0_attn_a_in['dt_proj_w'], 'L0_attn_a_dt_proj_b': _L0_attn_a_in['dt_proj_b'], 'L0_attn_a_A_log': _L0_attn_a_in['A_log'], 'L0_attn_a_Dskip': _L0_attn_a_in['Dskip'], 'L0_attn_a_out_proj_w': _L0_attn_a_in['out_proj_w'], 'L0_attn_a_ln_w': _L0_attn_a_in['ln_w'], 'L0_attn_a_ln_b': _L0_attn_a_in['ln_b'], 'L0_attn_b_W_kqv': _L0_attn_b_in['W_kqv'], 'L0_attn_b_b_kqv': _L0_attn_b_in['b_kqv'], 'L0_attn_b_W_proj': _L0_attn_b_in['W_proj'], 'L0_attn_b_b_proj': _L0_attn_b_in['b_proj'], 'L0_attn_b_slopes': _L0_attn_b_in['slopes'], 'L0_ffn_Ws': _L0_ffn_in['Ws'], 'L0_ffn_bs': _L0_ffn_in['bs'], 'L0_ffn_Wg': _L0_ffn_in['Wg'], 'L0_ffn_Wu': _L0_ffn_in['Wu'], 'L0_ffn_Wd': _L0_ffn_in['Wd']}
    _x0 = _d['L0_attn_a_x']
    _d['L0_attn_a_x'] = jax.random.normal(jax.random.fold_in(jax.random.key(seed), 1), (8, 512, 128), dtype=_x0.dtype)
    del _x0
    return _d

def reference(L0_attn_a_x, L0_attn_a_in_proj_w, L0_attn_a_conv_w, L0_attn_a_conv_b, L0_attn_a_x_proj_w, L0_attn_a_dt_proj_w, L0_attn_a_dt_proj_b, L0_attn_a_A_log, L0_attn_a_Dskip, L0_attn_a_out_proj_w, L0_attn_a_ln_w, L0_attn_a_ln_b, L0_attn_b_W_kqv, L0_attn_b_b_kqv, L0_attn_b_W_proj, L0_attn_b_b_proj, L0_attn_b_slopes, L0_ffn_Ws, L0_ffn_bs, L0_ffn_Wg, L0_ffn_Wu, L0_ffn_Wd):

    def _L0_attn_a_ref(x, in_proj_w, conv_w, conv_b, x_proj_w, dt_proj_w, dt_proj_b, A_log, Dskip, out_proj_w, ln_w, ln_b):
        import jax, jax.numpy as jnp
        import numpy as np
        N_LAYERS = 2
        D_MODEL = 128
        D_STATE = 16
        D_CONV = 4
        EXPAND = 2
        D_INNER = EXPAND * D_MODEL
        DT_RANK = (D_MODEL + 15) // 16
        B, T = (2, 128)
        LN_EPS = 1e-05

        def _layer_norm(x, w, b):
            mu = jnp.mean(x, axis=-1, keepdims=True)
            xc = x - mu
            var = jnp.mean(xc * xc, axis=-1, keepdims=True)
            return xc * jax.lax.rsqrt(var + LN_EPS) * w + b

        def _mamba_layer(x, in_w, cw, cb, xp_w, dt_w, dt_b, A_log, Dskip, out_w):
            xz = jnp.einsum('btd,ed->bte', x, in_w)
            xc, z = jnp.split(xz, 2, axis=-1)
            pad = D_CONV - 1
            xpad = jnp.pad(xc, ((0, 0), (pad, 0), (0, 0)))
            Tlen = xc.shape[1]
            conv = sum((xpad[:, k:k + Tlen, :] * cw[:, k] for k in range(D_CONV))) + cb
            u = jax.nn.silu(conv)
            x_dbl = jnp.einsum('btd,ed->bte', u, xp_w)
            dt, Bm, Cm = jnp.split(x_dbl, [DT_RANK, DT_RANK + D_STATE], axis=-1)
            dt = jax.nn.softplus(jnp.einsum('btr,dr->btd', dt, dt_w) + dt_b)
            A = -jnp.exp(A_log)

            def step(h, inp):
                dt_t, B_t, C_t, u_t = inp
                dA = jnp.exp(dt_t[:, :, None] * A)
                h = dA * h + (dt_t * u_t)[:, :, None] * B_t[:, None, :]
                y = jnp.einsum('bdn,bn->bd', h, C_t)
                return (h, y)
            h0 = jnp.zeros((x.shape[0], D_INNER, D_STATE), x.dtype)
            _, ys = jax.lax.scan(step, h0, (dt.transpose(1, 0, 2), Bm.transpose(1, 0, 2), Cm.transpose(1, 0, 2), u.transpose(1, 0, 2)))
            y = ys.transpose(1, 0, 2) + u * Dskip
            y = y * jax.nn.silu(z)
            return jnp.einsum('bti,oi->bto', y, out_w)
        for l in range(N_LAYERS):
            residual = x
            h = _mamba_layer(x, in_proj_w[l], conv_w[l], conv_b[l], x_proj_w[l], dt_proj_w[l], dt_proj_b[l], A_log[l], Dskip[l], out_proj_w[l])
            h = _layer_norm(h, ln_w[l], ln_b[l])
            x = h + residual
        return x

    def _L0_attn_b_ref(x, W_kqv, b_kqv, W_proj, b_proj, slopes):
        import jax, jax.numpy as jnp
        import numpy as np
        B, S, E, H = (2, 256, 128, 16)
        D = E // H
        NEG_INF = -1e+30

        def alibi_slopes(n_head):
            return jnp.asarray([2.0 ** (-8.0 * (i + 1) / n_head) for i in range(n_head)], dtype=jnp.float32)
        b, s, e = x.shape
        kqv = x @ W_kqv + b_kqv
        k, q, v = jnp.split(kqv, 3, axis=-1)
        k = k.reshape(b, s, H, D)
        q = q.reshape(b, s, H, D)
        v = v.reshape(b, s, H, D)
        attn = jnp.einsum('bqhd,bkhd->bhqk', q, k) * (1.0 / jnp.sqrt(jnp.float32(D)))
        i = jnp.arange(s)[:, None]
        j = jnp.arange(s)[None, :]
        rel = (j - i).astype(jnp.float32)
        bias = slopes[:, None, None] * jnp.tril(rel)
        bias = jnp.where(j > i, NEG_INF, bias)
        attn = jax.nn.softmax(attn + bias[None], axis=-1)
        y = jnp.einsum('bhqk,bkhd->bqhd', attn, v).reshape(b, s, e)
        return y @ W_proj + b_proj

    def _L0_ffn_ref(x, Ws, bs, Wg, Wu, Wd):
        import jax, jax.numpy as jnp
        import numpy as np
        D, F, E, K = (128, 344, 8, 2)
        b, n, d = x.shape
        xt = x.reshape(-1, d)
        logits = xt @ Ws + bs
        topk_w, topk_idx = jax.lax.top_k(logits, K)
        topk_w = jax.nn.softmax(topk_w, axis=-1)
        combine = jnp.sum(jax.nn.one_hot(topk_idx, E, dtype=xt.dtype) * topk_w[..., None], axis=1)
        g = jnp.einsum('td,edf->tef', xt, Wg)
        u = jnp.einsum('td,edf->tef', xt, Wu)
        h = jax.nn.silu(g) * u
        y = jnp.einsum('tef,efd->ted', h, Wd)
        out = jnp.einsum('ted,te->td', y, combine)
        return out.reshape(b, n, d)
    x = L0_attn_a_x
    x = x + _L0_attn_a_ref(_layernorm(x, axis=-1), L0_attn_a_in_proj_w, L0_attn_a_conv_w, L0_attn_a_conv_b, L0_attn_a_x_proj_w, L0_attn_a_dt_proj_w, L0_attn_a_dt_proj_b, L0_attn_a_A_log, L0_attn_a_Dskip, L0_attn_a_out_proj_w, L0_attn_a_ln_w, L0_attn_a_ln_b)
    x = x + _L0_ffn_ref(_layernorm(x, axis=-1), L0_ffn_Ws, L0_ffn_bs, L0_ffn_Wg, L0_ffn_Wu, L0_ffn_Wd)
    x = x + _L0_attn_b_ref(_layernorm(x, axis=-1), L0_attn_b_W_kqv, L0_attn_b_b_kqv, L0_attn_b_W_proj, L0_attn_b_b_proj, L0_attn_b_slopes)
    x = x + _L0_ffn_ref(_layernorm(x, axis=-1), L0_ffn_Ws, L0_ffn_bs, L0_ffn_Wg, L0_ffn_Wu, L0_ffn_Wd)
    return x

_drawn_inputs = setup_inputs


def setup_inputs(seed=0):
    import zlib

    import numpy as np

    out = dict(_drawn_inputs(seed))
    spreads = {'L0_attn_a_conv_b': (0.0, 0.1),
     'L0_attn_a_dt_proj_b': (-4.599999904632568, 0.6),
     'L0_attn_a_Dskip': (1.0, 0.2),
     'L0_attn_a_ln_w': (1.0, 0.2),
     'L0_attn_a_ln_b': (0.0, 0.1),
     'L0_attn_b_b_kqv': (0.0, 0.745),
     'L0_attn_b_b_proj': (0.0, 0.1),
     'L0_ffn_bs': (0.0, 0.8)}
    factors = {'L0_attn_a_x_proj_w': 8.0,
     'L0_attn_a_dt_proj_w': 34.087,
     'L0_attn_a_A_log': 8.0,
     'L0_attn_b_W_kqv': 8.0,
     'L0_attn_b_W_proj': 4.611,
     'L0_attn_b_slopes': 8.0,
     'L0_ffn_Ws': 8.0,
     'L0_ffn_Wg': 8.0,
     'L0_ffn_Wu': 8.0,
     'L0_ffn_Wd': 8.0}
    for name, (base, spread) in spreads.items():
        noise = np.random.default_rng([zlib.crc32(name.encode()), seed]).standard_normal(out[name].shape)
        drawn = base * np.exp(spread * noise) if base else spread * noise
        out[name] = jnp.asarray(drawn.astype(out[name].dtype))
    for name, factor in factors.items():
        out[name] = (out[name] * factor).astype(out[name].dtype)
    return out
```

```python
from contextlib import ExitStack

import concourse.bass as bass
from concourse import mybir
from concourse.alu_op_type import AluOpType as ALU

F32 = mybir.dt.float32
F32R = mybir.dt.float32r
U32 = mybir.dt.uint32
ACT = mybir.ActivationFunctionType
AX = mybir.AxisListType
EPS = 1e-5

B, T, D = 8, 512, 128
P = 128
S = T // P
L = 2
DI, H = 256, 2
NS, R, KC = 16, 8, 4
QUAD = 4
UNITS = QUAD * L
BLK = S * D


def hold(e, s, v, held):
    e.wait_ge(s, v)
    e.sem_inc(held, 1)


class LayerNorm:
    NDVE, NACT = 16, 2

    def __init__(self, name, sb, sem, held, base=0):
        self.held = held
        self.base = base
        self.st = sb(name + "_bn", [P, S, 6])
        self.mv = sb(name + "_mean_var", [P, S, 2])
        self.r = sb(name + "_rstd", [P, 4, S])
        self.eps = sb(name + "_eps", [P, 1])
        self.dve_done, self.act_done = sem(name + "_dve"), sem(name + "_act")

    def setup(self, e):
        return e.memset(self.eps[:], EPS)

    def stats(self, e, v, src):
        for s in range(S):
            e.bn_stats(self.st[:, s, :], src(s)).then_inc(self.dve_done, 1)
        for s in range(S):
            hold(e, self.dve_done, v * self.NDVE + self.base + (1 + s), self.held)
            e.bn_aggr(self.mv[:, s, :], self.st[:, s, :]).then_inc(self.dve_done, 1)

    def act(self, e, v):
        e.wait_ge(self.dve_done, v * self.NDVE + self.base + 8)
        e.activation(self.r[:, 0, :], self.mv[:, :, 1], ACT.Ln, bias=self.eps[:, 0:1]).then_inc(self.act_done, 1)
        e.wait_ge(self.act_done, v * self.NACT + 1)
        e.activation(self.r[:, 1, :], self.r[:, 0, :], ACT.Exp, scale=-0.5).then_inc(self.act_done, 1)

    def apply(self, e, v, src, dst):
        r, r2, t = self.r[:, 1, :], self.r[:, 2, :], self.r[:, 3, :]
        at = lambda n: e.wait_ge(self.dve_done, v * self.NDVE + self.base + n)
        e.wait_ge(self.act_done, v * self.NACT + 2)
        e.tensor_tensor(r2, r, r, ALU.mult).then_inc(self.dve_done, 1)
        at(9)
        e.scalar_tensor_tensor(t, self.mv[:, :, 1], EPS, r2, ALU.add, ALU.mult).then_inc(self.dve_done, 1)
        at(10)
        e.tensor_scalar(t, t, -0.5, 1.5, ALU.mult, ALU.add).then_inc(self.dve_done, 1)
        at(11)
        e.tensor_tensor(r2, r, t, ALU.mult).then_inc(self.dve_done, 1)
        at(12)
        for s in range(S):
            e.tensor_scalar(dst(s), src(s), self.mv[:, s, 0:1], r2[:, s:s + 1], ALU.subtract, ALU.mult)\
                .then_inc(self.dve_done, 1)


def mamba_phase(sb, psum, sem, held, X, w, ident, loaded, loads):
    a = sb("decay", [P, 3, H * T])
    g = sb("drive", [P, 3, H * T])
    h = sb("state", [P, 3, H * T])
    hc = sb("state_c", [P, 2, H * T])
    bsb = sb("b_rows", [P, 3, T])
    u = sb("u", [P, 2, H * T])
    sz = sb("silu_z", [P, 2, H * T])
    dt = sb("dt", [P, 2, H * T])
    dtu = sb("dtu", [P, 2, H * T])
    xcp = sb("xc_padded", [P, H, KC - 1 + T])
    cv = sb("conv", [P, H * T])
    t1 = sb("t1", [P, H * T])
    t2 = sb("t2", [P, H * T])
    t3 = sb("t3", [P, H * T])
    yg = sb("y_gated", [P, H * T])
    xT = sb("xT", [P, T])
    bc = sb("bc_split", [64, 2, T], F32R)
    dtr = sb("dt_low_rank", [64, T])
    zs = sb("z_stage", [P, QUAD, S * D])
    hn = sb("normed", [P, S * D])
    sel = sb("row_select", [64, 2 * NS, P], F32R)
    Aneg = sb("a_neg", [P, L, H, NS])

    PB = [psum(f"rep_b{j}", [P, T]) for j in range(2)]
    PC = [psum(f"rep_c{j}", [P, T]) for j in range(2)]
    Y = [psum(f"y{j}", [P, T]) for j in range(H)]
    S0, S1 = psum("s0", [P, T]), psum("s1", [P, T])

    CREDIT = 40
    rep_b_done = sem("rep_b_done")
    rep_c_done = sem("rep_c_done")
    bcopy_done = sem("bcopy_done")
    exp_done = sem("exp_done")
    drive_done = sem("drive_done")
    scan_done = sem("scan_done")
    cmul_done = sem("cmul_done")
    nsum_done = sem("nsum_done")
    pre_pe, pre_act, pre_dve, pre_pool = sem("pre_pe"), sem("pre_act"), sem("pre_dve"), sem("pre_pool")
    post_pe, post_act, post_dve, post_pool = sem("post_pe"), sem("post_act"), sem("post_dve"), sem("post_pool")
    setup = sem("mamba_setup")
    ln_in = LayerNorm("ln_in", sb, sem, held)
    ln_out = LayerNorm("ln_out", sb, sem, held, CREDIT)
    NPE, NACT, NDVE = 8, 16, 9
    QPE, QDVE = 1, 3
    POST_POOL = [0, 3, 6, 9, 12, 16, 20, 24]
    QPOOL = 28

    class At:
        def __init__(self, i, k):
            self.i, self.k, self.q, self.l = i, k % UNITS, k % 2, (k % UNITS) // QUAD
            self.z = k % QUAD

        def step(self, n, per=1):
            return self.i * (UNITS * NS * per) + (self.k * NS * per + n * per)

        def count(self, per, n):
            return self.i * (UNITS * per) + (self.k * per + n)

    def wait(e, s, v):
        e.wait_ge(s, v + CREDIT)

    def wait_post_norm(e, c):
        back = 2 if c.k == 1 else 3
        e.wait_ge(ln_out.dve_done, c.count(LayerNorm.NDVE, (1 - back) * LayerNorm.NDVE) + CREDIT)

    def pe_tr(e, c):
        if c.l == 0:
            e.wait_ge(ln_in.dve_done, (c.i * QUAD + c.z) * LayerNorm.NDVE + 16)
        else:
            wait(e, post_pool, c.i * QPOOL + 3 * (c.z + 1))
        wait(e, pre_act, c.count(NACT, -NACT + 12))
        for s in range(S):
            m = e.transpose(S0[:, s * P:(s + 1) * P], zs[:, c.z, s * D:(s + 1) * D], ident[:])
        m.then_inc(pre_pe, 1)

    def pe_inproj(e, c, j):
        if True:
            out = S1 if j % 2 == 0 else S0
            if j == 0:
                wait(e, pre_act, c.count(NACT, 1))
                wait_post_norm(e, c)
            elif j > 1:
                wait(e, pre_act, c.count(NACT, j))
            e.matmul(out[:], w["in"][:, c.l, j * P:(j + 1) * P], xT[:], start=True, stop=True).then_inc(pre_pe, 1)

    def pe_xproj(e, c):
        wait(e, pre_act, c.count(NACT, 8))
        for hh in range(H):
            m = e.matmul(S1[0:40, :], w["xp"][:, c.l, hh, :], u[:, c.q, hh * T:(hh + 1) * T],
                         start=(hh == 0), stop=(hh == H - 1))
        m.then_inc(pre_pe, 1)

    def pe_dtproj(e, c):
        wait(e, pre_act, c.count(NACT, 10))
        for hh in range(H):
            if hh == 1:
                wait(e, pre_dve, c.count(NDVE, 7))
            e.matmul((S0, S1)[hh][:], w["dt"][32:40, c.l, hh * P:(hh + 1) * P], dtr[32:40, :],
                     start=True, stop=True).then_inc(pre_pe, 1)

    def pe_out(e, c, latest):
        wait(e, pre_act, latest.count(NACT, 14))
        wait(e, post_dve, c.count(QDVE, 3))
        for s in range(S):
            for hh in range(H):
                m = e.matmul(S1[:, s * D:(s + 1) * D], yg[:, hh * T + s * P:hh * T + (s + 1) * P],
                             w["out"][:, c.l, hh, :], start=(hh == 0), stop=(hh == H - 1))
        m.then_inc(post_pe, 1)

    def pe_steps(e, c, hooks):
        def nsum(n):
            wait(e, cmul_done, c.step(n + 1))
            if n == 0:
                wait(e, post_dve, c.count(QDVE, -QDVE + 2))
            for hh in range(H):
                m = e.matmul(Y[hh][:], ident[:], hc[:, n % 2, hh * T:(hh + 1) * T],
                             start=(n == 0), stop=(n == NS - 1))
            m.then_inc(nsum_done, 1)

        def rep_b(n):
            wait(e, bcopy_done, c.step(n - 1))
            e.matmul(PB[n % 2][:], sel[:, n, :], bc[:, c.q, :], start=True, stop=True).then_inc(rep_b_done, 1)

        def rep_c(n):
            wait(e, cmul_done, c.step(n - 1))
            e.matmul(PC[n % 2][:], sel[:, NS + n, :], bc[:, c.q, :], start=True, stop=True).then_inc(rep_c_done, 1)

        wait(e, pre_dve, c.count(NDVE, 7))
        rep_b(0)
        rep_b(1)
        rep_c(0)
        for n in range(NS):
            if n + 2 < NS:
                rep_b(n + 2)
            if n + 1 < NS:
                rep_c(n + 1)
            if n >= 1:
                nsum(n - 1)
            hooks(n)
        nsum(NS - 1)

    def act_pre_a(e, c):
        wait(e, pre_pe, c.count(NPE, 1))
        e.activation(xT[:], S0[:], ACT.Copy).then_inc(pre_act, 1)

    def act_pre_xc(e, c):
        for hh in range(H):
            wait(e, pre_pe, c.count(NPE, 2 + hh))
            e.activation(xcp[:, hh, KC - 1:], (S1, S0)[hh][:], ACT.Copy).then_inc(pre_act, 1)
        wait(e, pre_act, c.count(NACT, 3))
        for hh in range(H):
            e.activation(cv[:, hh * T:(hh + 1) * T], xcp[:, hh, 0:T], ACT.Identity,
                         bias=w["cb"][:, c.l, hh:hh + 1], scale=w["cw"][:, c.l, hh, 0:1]).then_inc(pre_act, 1)

    def act_pre_b(e, c):
        wait(e, post_dve, c.count(QDVE, -2 * QDVE + 3))
        for hh in range(H):
            wait(e, pre_pe, c.count(NPE, 4 + hh))
            e.activation(sz[:, c.q, hh * T:(hh + 1) * T], (S1, S0)[hh][:], ACT.Silu).then_inc(pre_act, 1)
        wait(e, pre_dve, c.count(NDVE, 6))
        e.activation(u[:, c.q, :], cv[:], ACT.Silu).then_inc(pre_act, 1)
        e.preload_act_table_set("natural_log_exp_and_others")

    def act_pre_c(e, c):
        wait(e, pre_pe, c.count(NPE, 6))
        e.activation(bc[0:32, c.q, :], S1[0:32, :], ACT.Copy).then_inc(pre_act, 1)
        e.activation(dtr[32:40, :], S1[32:40, :], ACT.Copy).then_inc(pre_act, 1)

    def act_pre_d(e, c):
        for hh in range(H):
            part = slice(hh * T, (hh + 1) * T)
            wait(e, pre_pe, c.count(NPE, 7 + hh))
            e.activation(t1[:, part], (S0, S1)[hh][:], ACT.Abs, bias=w["dtb"][:, c.l, hh:hh + 1]).then_inc(pre_act, 1)
            e.activation(t3[:, part], (S0, S1)[hh][:], ACT.Relu, bias=w["dtb"][:, c.l, hh:hh + 1]).then_inc(pre_act, 1)
        wait(e, pre_act, c.count(NACT, 13))
        e.activation(t2[:], t1[:], ACT.Exp, scale=-1.0).then_inc(pre_act, 1)
        wait(e, pre_act, c.count(NACT, 15))
        e.activation(t1[:], t2[:], ACT.Ln, bias=1.0).then_inc(pre_act, 1)

    def act_ln_in(e, c):
        ln_in.act(e, c.i * QUAD + c.z)

    def act_post(e, c):
        ln_out.act(e, c.unit)

    def act_steps(e, c, hooks):
        def copy_b(n):
            wait(e, rep_b_done, c.step(n + 1))
            wait(e, drive_done, c.step(n - 2))
            e.activation(bsb[:, n % 3, :], PB[n % 2][:], ACT.Copy).then_inc(bcopy_done, 1)

        copy_b(0)
        for n in range(NS):
            if n + 1 < NS:
                copy_b(n + 1)
            if n == 0:
                wait(e, pre_dve, c.count(NDVE, 8))
            wait(e, scan_done, c.step(n - 2))
            for hh in range(H):
                m = e.activation(a[:, n % 3, hh * T + 1:(hh + 1) * T], dt[:, c.q, hh * T + 1:(hh + 1) * T],
                                 ACT.Exp, scale=Aneg[:, c.l, hh, n:n + 1])
            m.then_inc(exp_done, 1)
            hooks(n)

    def two(ap):
        return ap.rearrange("p (o t) -> p o t", o=1).to_broadcast([P, H, T])

    def halves(ap):
        return ap.rearrange("p (h t) -> p h t", h=H)

    def pool_steps(e, c, hooks):
        for n in range(NS):
            if n == 0:
                wait(e, pre_dve, c.count(NDVE, 9))
            wait(e, bcopy_done, c.step(n + 1))
            wait(e, scan_done, c.step(n - 2))
            e.tensor_tensor(halves(g[:, n % 3, :]), halves(dtu[:, c.q, :]), two(bsb[:, n % 3, :]),
                            ALU.mult).then_inc(drive_done, 1)
            hooks(n)

    def pool_post(e, c):
        base = c.i * QPOOL + POST_POOL[c.k]
        v = lambda ap: ap.rearrange("p (s d) -> p s d", s=S)
        over = lambda ap: ap.rearrange("p (o d) -> p o d", o=1).to_broadcast([P, S, D])
        e.wait_ge(ln_out.dve_done, c.unit * LayerNorm.NDVE + 16 + CREDIT)
        e.tensor_tensor(v(hn[:]), v(hn[:]), over(w["lnw"][:, c.l, :]), ALU.mult).then_inc(post_pool, 1)
        wait(e, post_pool, base + 1)
        e.tensor_tensor(v(hn[:]), v(hn[:]), over(w["lnb"][:, c.l, :]), ALU.add).then_inc(post_pool, 1)
        wait(e, post_pool, base + 2)
        if c.l == 0:
            e.tensor_tensor(zs[:, c.z, :], zs[:, c.z, :], hn[:], ALU.add).then_inc(post_pool, 1)
            wait(e, post_pool, base + 3)
        else:
            e.tensor_tensor(hn[:], zs[:, c.z, :], hn[:], ALU.add).then_inc(post_pool, 1)
            wait(e, post_pool, base + 3)
            xb = X[:, bass.ds(c.batch * (S * D), S * D)]
            e.tensor_tensor(xb, xb, hn[:], ALU.add).then_inc(post_pool, 1)
            wait(e, post_pool, base + 4)

    def dve_conv(e, c, k):
        for hh in range(H):
            part = slice(hh * T, (hh + 1) * T)
            if k == 1:
                wait(e, pre_act, c.count(NACT, 4 + hh))
            else:
                wait(e, pre_dve, c.count(NDVE, 2 * (k - 2) + hh + 1))
            e.scalar_tensor_tensor(cv[:, part], xcp[:, hh, k:k + T], w["cw"][:, c.l, hh, k:k + 1], cv[:, part],
                                   ALU.mult, ALU.add).then_inc(pre_dve, 1)

    def dve_bc(e, c):
        wait(e, pre_act, c.count(NACT, 9))
        e.tensor_tensor(bc[32:64, c.q, :], S1[0:32, :], bc[0:32, c.q, :].bitcast(F32), ALU.subtract)\
            .then_inc(pre_dve, 1)

    def dve_dt(e, c):
        wait(e, pre_act, c.count(NACT, 16))
        e.tensor_tensor(dt[:, c.q, :], t1[:], t3[:], ALU.add).then_inc(pre_dve, 1)
        wait(e, pre_dve, c.count(NDVE, 8))
        e.tensor_tensor(dtu[:, c.q, :], dt[:, c.q, :], u[:, c.q, :], ALU.mult).then_inc(pre_dve, 1)

    def dve_post_a(e, c):
        wait(e, nsum_done, c.step(NS))
        for hh in range(H):
            part = slice(hh * T, (hh + 1) * T)
            e.scalar_tensor_tensor(yg[:, part], u[:, c.q, part], w["D"][:, c.l, hh:hh + 1], Y[hh][:],
                                   ALU.mult, ALU.add).then_inc(post_dve, 1)
        wait(e, post_dve, c.count(QDVE, 2))
        e.tensor_tensor(yg[:], yg[:], sz[:, c.q, :], ALU.mult).then_inc(post_dve, 1)

    def dve_post_b(e, c):
        wait(e, post_pe, c.count(QPE, 1))
        ln_out.stats(e, c.unit, lambda s: S1[:, s * D:(s + 1) * D])

    def dve_post_c(e, c):
        wait(e, post_pool, c.i * QPOOL + POST_POOL[c.k])
        ln_out.apply(e, c.unit, lambda s: S1[:, s * D:(s + 1) * D], lambda s: hn[:, s * D:(s + 1) * D])

    def x_block(c, s):
        return X[:, bass.ds(c.batch * BLK + s * D, D)]

    def dve_ln_in_a(e, c):
        ln_in.stats(e, c.i * QUAD + c.z, lambda s: x_block(c, s))

    def dve_ln_in_b(e, c):
        wait(e, post_pool, (c.i - 1) * QPOOL + POST_POOL[QUAD] + 4 * (c.z + 1))
        ln_in.apply(e, c.i * QUAD + c.z, lambda s: x_block(c, s), lambda s: zs[:, c.z, s * D:(s + 1) * D])

    def dve_steps(e, c, hooks):
        def cmul(n):
            wait(e, rep_c_done, c.step(n + 1))
            wait(e, scan_done, c.step(n + 1))
            wait(e, nsum_done, c.step(n - 1))
            e.tensor_tensor(halves(hc[:, n % 2, :]), halves(h[:, n % 3, :]), two(PC[n % 2][:]),
                            ALU.mult).then_inc(cmul_done, 1)

        for n in range(NS):
            wait(e, exp_done, c.step(n + 1))
            wait(e, drive_done, c.step(n + 1))
            wait(e, cmul_done, c.step(n - 2))
            e.tensor_tensor_scan(h[:, n % 3, :], a[:, n % 3, :], g[:, n % 3, :], 0.0, ALU.mult, ALU.add)\
                .then_inc(scan_done, 1)
            if n >= 1:
                cmul(n - 1)
            hooks(n)
        cmul(NS - 1)

    def arg(f, j):
        return lambda e, c: f(e, c, j)

    PIECES = {
        "pe": [(0, "pre", pe_tr), (2, "pre", arg(pe_inproj, 0)), (3, "pre", arg(pe_inproj, 1)),
               (5, "pre", arg(pe_inproj, 2)), (6, "pre", arg(pe_inproj, 3)), (8, "pre", pe_xproj),
               (10, "pre", pe_dtproj), (12, "post", pe_out)],
        "act": [(2, "pre", act_pre_a), (5, "pre", act_pre_xc), (8, "pre", act_pre_b), (10, "pre", act_pre_c),
                (12, "pre", act_pre_d), (13, "ln_in", act_ln_in), (15, "post", act_post)],
        "dve": [(0, "post", dve_post_a), (5, "pre", arg(dve_conv, 1)), (6, "pre", arg(dve_conv, 2)),
                (7, "pre", arg(dve_conv, 3)), (9, "pre", dve_bc), (11, "ln_in", dve_ln_in_a),
                (13, "pre", dve_dt), (13, "ln_in", dve_ln_in_b), (14, "post", dve_post_b), (15, "post", dve_post_c)],
        "pool": [(15, "post", pool_post)],
    }
    STEPS = {"pe": pe_steps, "act": act_steps, "dve": dve_steps, "pool": pool_steps}

    def unit(i, k):
        c = At(i if k < UNITS else i + 1, k)
        c.batch = c.i * QUAD + c.z
        c.unit = c.i * UNITS + c.k
        return c

    def piece(e, f, c, latest):
        f(e, c, latest) if f is pe_out else f(e, c)

    def program(e, which):
        for kind_now, c in (("ln_in", unit(0, 0)), ("ln_in", unit(0, 1)), ("pre", unit(0, 0))):
            for _, kind, f in PIECES[which]:
                if kind == kind_now:
                    f(e, c)
        with e.Fori(0, B // QUAD) as i:
            for k in range(UNITS):
                c, nxt, after = unit(i, k), unit(i, k + 1), unit(i, k + 2)
                post = unit(i, k - 1) if k else None

                def hooks(n):
                    for at, kind, f in PIECES[which]:
                        if at != n:
                            continue
                        if kind == "pre":
                            f(e, nxt)
                        elif kind == "ln_in" and after.l == 0:
                            f(e, after)
                        elif kind == "post" and post is not None:
                            piece(e, f, post, nxt)

                STEPS[which](e, c, hooks)
            for _, kind, f in PIECES[which]:
                if kind == "post":
                    piece(e, f, unit(i, UNITS - 1), unit(i, UNITS))

    def dve_setup(e):
        e.memset(a[:].rearrange("p s (h t) -> p (s h) t", h=H)[:, :, 0:1], 0.0).then_inc(setup, 1)
        e.memset(xcp[:, :, 0:KC - 1], 0.0).then_inc(setup, 1)
        e.memset(X[:, B * BLK:], 0.0).then_inc(setup, 1)
        ln_in.setup(e).then_inc(setup, 1)
        ln_out.setup(e).then_inc(setup, 1)
        for s in (scan_done, cmul_done, pre_dve, post_dve, ln_out.dve_done):
            e.sem_inc(s, CREDIT)
        e.wait_ge(loaded, 16 * loads)
        e.tensor_copy(sel[:], w["id2"][:, :].rearrange("p (n o) -> p n o", o=1).to_broadcast([64, 2 * NS, P]))\
            .then_inc(setup, 1)
        e.wait_ge(setup, 7)
        e.tensor_scalar(Aneg[:], Aneg[:], -1.0, None, ALU.mult).then_inc(setup, 1)

    def act_setup(e):
        for s in (bcopy_done, exp_done, pre_act):
            e.sem_inc(s, CREDIT)
        e.wait_ge(loaded, 16 * loads)
        e.preload_act_table_set("natural_log_exp_and_others")
        e.activation(Aneg[:], w["alog"][:], ACT.Exp).then_inc(setup, 1)
        e.wait_ge(setup, 8)

    def pe_setup(e):
        for s in (rep_b_done, rep_c_done, nsum_done, pre_pe, post_pe):
            e.sem_inc(s, CREDIT)
        e.wait_ge(loaded, 16 * loads)
        e.wait_ge(setup, 8)

    def pool_setup(e):
        for s in (drive_done, post_pool):
            e.sem_inc(s, CREDIT)
        e.wait_ge(loaded, 16 * loads)
        e.wait_ge(setup, 8)

    setups = {"pe": pe_setup, "act": act_setup, "dve": dve_setup, "pool": pool_setup}

    def run(e, which):
        setups[which](e)
        if which == "dve":
            e.wait_ge(setup, 8)
        program(e, which)

    return run


E_, F_ = 8, 344
HT = [128, 128, F_ - 256]
WCOL = 2 * F_ + 3 * D
HEADS, DH = 16, 8
GROUPS = 4
NEG = -1e30


def f32(ap):
    return ap.bitcast(F32)


def barrier(e, phase_end, n):
    e.drain().then_inc(phase_end, 1)
    e.wait_ge(phase_end, 4 * n)


def ffn_phase(sb, psum, sem, held, X, ident, wh, wl, ws, bs, iota8, sel8):
    CREDIT = 80
    NM = 3 * E_
    ln = LayerNorm("ffn_ln", sb, sem, held)
    xn = sb("ffn_xn", [P, BLK])
    xf = sb("ffn_xT", [P, T])
    xh = sb("ffn_xT_hi", [P, 2, T], F32R)
    xl = sb("ffn_xT_lo", [P, 2, T], F32R)
    lg = sb("logits", [P, S, E_])
    top = sb("top", [P, S, 8])
    idx = sb("top_index", [P, S, 8], U32)
    idf = sb("top_index_f", [P, S, 2])
    wt = sb("top_weight", [P, 5, S, 1])
    cmb = sb("combine", [P, 2, S, E_])
    ch = sb("combine_hi", [E_, 2, T], F32R)
    cl = sb("combine_lo", [E_, 2, T], F32R)
    sg = sb("silu_gate", [P, 2, T])
    hf = sb("hidden", [P, 3, T])
    hh = sb("hidden_hi", [P, 3, T], F32R)
    hl = sb("hidden_lo", [P, 3, T], F32R)
    cbs = sb("combine_rows", [P, 2, T])
    ot = sb("expert_out", [P, 2, T])
    ya = sb("ffn_acc", [P, 2, T])
    G = [psum(f"gate{j}", [P, T]) for j in range(2)]
    U = [psum(f"up{j}", [P, T]) for j in range(2)]
    O = [psum(f"down{j}", [P, T]) for j in range(2)]
    CB = psum("combine_ps", [P, T])
    M = psum("ffn_pre_ps", [P, T])
    gate_done, up_done, down_done, cb_done, ytr_done = (sem(n) for n in (
        "gate_done", "up_done", "down_done", "cb_done", "ytr_done"))
    silu_done, hi_done, cbcopy_done = sem("silu_done"), sem("hi_done"), sem("cbcopy_done")
    prod_done, oscale_done, xadd_done = sem("prod_done"), sem("oscale_done"), sem("xadd_done")
    lo_done, yadd_done = sem("lo_done"), sem("yadd_done")
    fpre_pe, fpre_act, fpre_dve, ffn_setup = (sem(n) for n in ("fpre_pe", "fpre_act", "fpre_dve", "ffn_setup"))
    PPE, PACT, PDVE = 3, 4, 17

    class Tile:
        def __init__(self, f, i, k):
            self.b = i * 2 + k
            self.q = k % 2
            self.t = self.b + f * B
            self.p = self.b + f * (B + 1)

    def wait(e, s, v):
        e.wait_ge(s, v + CREDIT)

    def xsrc(c):
        return lambda s: X[:, bass.ds(c.b * BLK + s * D, D)]

    def dve_norm_a(e, c):
        ln.stats(e, c.p, xsrc(c))

    def act_norm(e, c):
        ln.act(e, c.p)

    def dve_norm_b(e, c):
        ln.apply(e, c.p, xsrc(c), lambda s: xn[:, s * D:(s + 1) * D])

    def pe_xtr(e, c):
        e.wait_ge(ln.dve_done, c.p * LayerNorm.NDVE + 16)
        wait(e, fpre_act, c.p * PACT)
        wait(e, fpre_dve, c.p * PDVE)
        for s in range(S):
            m = e.transpose(M[:, s * P:(s + 1) * P], xn[:, s * D:(s + 1) * D], ident[:])
        m.then_inc(fpre_pe, 1)

    def act_x(e, c):
        wait(e, fpre_pe, c.p * PPE + 1)
        wait(e, up_done, (c.t - 1) * NM)
        e.activation(xh[:, c.q, :], M[:], ACT.Copy).then_inc(fpre_act, 1)
        e.activation(xf[:], M[:], ACT.Copy).then_inc(fpre_act, 1)

    def dve_x(e, c):
        wait(e, fpre_act, c.p * PACT + 2)
        e.tensor_tensor(xl[:, c.q, :], M[:], f32(xh[:, c.q, :]), ALU.subtract).then_inc(fpre_dve, 1)

    def pe_logits(e, c):
        wait(e, fpre_dve, c.p * PDVE + 1)
        for s in range(S):
            m = e.matmul(M[:, s * E_:(s + 1) * E_], xf[:, s * P:(s + 1) * P], ws[:], start=True, stop=True)
        m.then_inc(fpre_pe, 1)

    def dve_route_a(e, c):
        base = c.p * PDVE
        wait(e, fpre_pe, c.p * PPE + 2)
        e.tensor_tensor(lg[:], M[:, 0:S * E_].rearrange("p (s n) -> p s n", s=S),
                        bs[:].rearrange("p (o n) -> p o n", o=1).to_broadcast([P, S, E_]), ALU.add)\
            .then_inc(fpre_dve, 1)
        hold(e, fpre_dve, base + 2 + CREDIT, held)
        for s in range(S):
            e.max(out=top[:, s, :], in_=lg[:, s, :]).then_inc(fpre_dve, 1)
        for s in range(S):
            hold(e, fpre_dve, base + 3 + s + CREDIT, held)
            e.max_index(out=idx[:, s, :], in_max=top[:, s, :], in_values=lg[:, s, :]).then_inc(fpre_dve, 1)
        wait(e, fpre_dve, base + 10)
        e.tensor_copy(idf[:], idx[:, :, 0:2]).then_inc(fpre_dve, 1)
        e.tensor_tensor(wt[:, 0], top[:, :, 1:2], top[:, :, 0:1], ALU.subtract).then_inc(fpre_dve, 1)

    def act_route(e, c):
        wait(e, fpre_dve, c.p * PDVE + 12)
        e.activation(wt[:, 1], wt[:, 0], ACT.Exp).then_inc(fpre_act, 1)

    def dve_route_b(e, c):
        base = c.p * PDVE
        it = iota8[:].rearrange("p (o n) -> p o n", o=1).to_broadcast([P, S, E_])
        wait(e, fpre_act, c.p * PACT + 3)
        e.tensor_scalar(wt[:, 2], wt[:, 1], 1.0, None, ALU.add).then_inc(fpre_dve, 1)
        wait(e, fpre_dve, base + 13)
        e.reciprocal(wt[:, 3], wt[:, 2]).then_inc(fpre_dve, 1)
        wait(e, fpre_dve, base + 14)
        e.tensor_tensor(wt[:, 4], wt[:, 3], wt[:, 1], ALU.mult).then_inc(fpre_dve, 1)
        wait(e, fpre_pe, (c.p - 1) * PPE + 3)
        e.tensor_tensor(cmb[:, 0], it, idf[:, :, 0:1].to_broadcast([P, S, E_]), ALU.is_equal).then_inc(xr, 1)
        e.tensor_tensor(cmb[:, 1], it, idf[:, :, 1:2].to_broadcast([P, S, E_]), ALU.is_equal).then_inc(xr, 1)
        wait(e, fpre_dve, base + 15)
        e.wait_ge(xr, c.p * 4 + 2)
        e.tensor_tensor(cmb[:, 0], cmb[:, 0], wt[:, 3].to_broadcast([P, S, E_]), ALU.mult).then_inc(xr, 1)
        e.tensor_tensor(cmb[:, 1], cmb[:, 1], wt[:, 4].to_broadcast([P, S, E_]), ALU.mult).then_inc(xr, 1)
        e.wait_ge(xr, c.p * 4 + 4)
        e.tensor_tensor(cmb[:, 0], cmb[:, 0], cmb[:, 1], ALU.add).then_inc(fpre_dve, 1)

    xr = sem("route_steps")

    def pe_ctr(e, c):
        wait(e, fpre_dve, c.p * PDVE + 16)
        for s in range(S):
            m = e.transpose(M[0:E_, s * P:(s + 1) * P], cmb[:, 0, s, :], ident[:])
        m.then_inc(fpre_pe, 1)

    def act_c(e, c):
        wait(e, fpre_pe, c.p * PPE + 3)
        wait(e, cb_done, (c.t - 1) * E_)
        e.activation(ch[:, c.q, :], M[0:E_, :], ACT.Copy).then_inc(fpre_act, 1)

    def dve_c(e, c):
        wait(e, fpre_act, c.p * PACT + 4)
        e.tensor_tensor(cl[:, c.q, :], M[0:E_, :], f32(ch[:, c.q, :]), ALU.subtract).then_inc(fpre_dve, 1)

    def part(m):
        return HT[m % 3]

    def three(e, out, w_sl, q, kind):
        e.matmul(out, wh(kind, w_sl), xh[:, q, :], start=True, stop=False)
        e.matmul(out, wl(kind, w_sl), xh[:, q, :], start=False, stop=False)
        return e.matmul(out, wh(kind, w_sl), xl[:, q, :], start=False, stop=True)

    def pe_tile(e, c, hooks):
        def down(m):
            j, ex = m % 3, m // 3
            rows = part(m)
            wait(e, hi_done, c.t * NM + m + 1)
            wait(e, lo_done, c.t * NM + m + 1)
            if j == 0:
                wait(e, oscale_done, c.t * E_ + ex - 1)
            out = O[ex % 2][:]
            e.matmul(out, wh("down", (ex, j, rows)), hh[0:rows, m % 3, :], start=(j == 0), stop=False)
            e.matmul(out, wl("down", (ex, j, rows)), hh[0:rows, m % 3, :], start=False, stop=False)
            e.matmul(out, wh("down", (ex, j, rows)), hl[0:rows, m % 3, :], start=False, stop=(j == 2))\
                .then_inc(down_done, 1)

        wait(e, fpre_dve, c.p * PDVE + 17)
        for m in range(NM):
            j, ex, rows = m % 3, m // 3, part(m)
            if j == 0:
                wait(e, cbcopy_done, c.t * E_ + ex)
                if ex == 0:
                    wait(e, xadd_done, c.t)
                e.matmul(CB[:], sel8[:, ex, :], ch[:, c.q, :], start=True, stop=False)
                e.matmul(CB[:], sel8[:, ex, :], cl[:, c.q, :], start=False, stop=True).then_inc(cb_done, 1)
            wait(e, silu_done, c.t * NM + m - 1)
            three(e, G[m % 2][0:rows, :], (ex, j, rows), c.q, "gate").then_inc(gate_done, 1)
            wait(e, prod_done, c.t * NM + m - 1)
            three(e, U[m % 2][0:rows, :], (ex, j, rows), c.q, "up").then_inc(up_done, 1)
            if m >= 2:
                down(m - 2)
            hooks(m)
        down(NM - 2)
        down(NM - 1)
        wait(e, yadd_done, c.t * E_ + E_)
        wait(e, cbcopy_done, c.t * E_ + E_)
        for s in range(S):
            m = e.transpose(CB[:, s * P:(s + 1) * P], ya[:, c.q, s * P:(s + 1) * P], ident[:])
        m.then_inc(ytr_done, 1)

    def act_tile(e, c, hooks):
        def hi(m):
            rows = part(m)
            wait(e, prod_done, c.t * NM + m + 1)
            wait(e, down_done, c.t * NM + m - 2)
            e.activation(hh[0:rows, m % 3, :], hf[0:rows, m % 3, :], ACT.Copy).then_inc(hi_done, 1)

        for m in range(NM):
            rows = part(m)
            wait(e, gate_done, c.t * NM + m + 1)
            wait(e, prod_done, c.t * NM + m - 1)
            e.activation(sg[0:rows, m % 2, :], G[m % 2][0:rows, :], ACT.Silu).then_inc(silu_done, 1)
            if m >= 1:
                hi(m - 1)
            if m % 3 == 1:
                ex = m // 3
                wait(e, cb_done, c.t * E_ + ex + 1)
                wait(e, oscale_done, c.t * E_ + ex - 1)
                e.activation(cbs[:, ex % 2, :], CB[:], ACT.Copy).then_inc(cbcopy_done, 1)
            hooks(m)
        hi(NM - 1)

    def dve_tile(e, c, hooks):
        def oscale(ex):
            wait(e, down_done, c.t * NM + 3 * ex + 3)
            wait(e, cbcopy_done, c.t * E_ + ex + 1)
            wait(e, yadd_done, c.t * E_ + ex - 1)
            e.tensor_tensor(ot[:, ex % 2, :], O[ex % 2][:], cbs[:, ex % 2, :], ALU.mult).then_inc(oscale_done, 1)

        for m in range(NM):
            rows = part(m)
            wait(e, silu_done, c.t * NM + m + 1)
            wait(e, up_done, c.t * NM + m + 1)
            wait(e, lo_done, c.t * NM + m - 2)
            e.tensor_tensor(hf[0:rows, m % 3, :], U[m % 2][0:rows, :], sg[0:rows, m % 2, :], ALU.mult)\
                .then_inc(prod_done, 1)
            if m >= 5 and m % 3 == 2:
                oscale((m - 5) // 3)
            hooks(m)
        oscale(E_ - 1)
        wait(e, ytr_done, c.t + 1)
        xb = X[:, bass.ds(c.b * BLK, BLK)]
        e.tensor_tensor(xb, xb, CB[:], ALU.add).then_inc(xadd_done, 1)

    def pool_tile(e, c, hooks):
        def yadd(ex):
            hold(e, oscale_done, c.t * E_ + ex + 1 + CREDIT, held)
            y = ya[:, c.q, :]
            if ex == 0:
                e.tensor_copy(y, ot[:, 0, :]).then_inc(yadd_done, 1)
            else:
                wait(e, yadd_done, c.t * E_ + ex)
                e.tensor_tensor(y, y, ot[:, ex % 2, :], ALU.add).then_inc(yadd_done, 1)

        for m in range(NM):
            rows = part(m)
            wait(e, hi_done, c.t * NM + m + 1)
            wait(e, down_done, c.t * NM + m - 2)
            e.tensor_tensor(hl[0:rows, m % 3, :], hf[0:rows, m % 3, :], f32(hh[0:rows, m % 3, :]), ALU.subtract)\
                .then_inc(lo_done, 1)
            if m >= 6 and m % 3 == 0:
                yadd((m - 6) // 3)
            hooks(m)
        yadd(E_ - 2)
        yadd(E_ - 1)

    PIECES = {
        "pe": [(9, pe_xtr), (12, pe_logits), (18, pe_ctr)],
        "act": [(8, act_norm), (11, act_x), (15, act_route), (20, act_c)],
        "dve": [(7, dve_norm_a), (8, dve_norm_b), (11, dve_x), (13, dve_route_a), (16, dve_route_b), (21, dve_c)],
        "pool": [],
    }
    TILES = {"pe": pe_tile, "act": act_tile, "dve": dve_tile, "pool": pool_tile}
    OWN = {"pe": (gate_done, up_done, down_done, cb_done, ytr_done, fpre_pe),
           "act": (silu_done, hi_done, cbcopy_done, fpre_act),
           "dve": (prod_done, oscale_done, xadd_done, fpre_dve), "pool": (lo_done, yadd_done)}

    def credits(e, which):
        for s in OWN[which]:
            e.sem_inc(s, CREDIT)

    def run(e, which, f):
        if which == "dve":
            ln.setup(e).then_inc(ffn_setup, 1)
        e.wait_ge(ffn_setup, f + 1)
        for _, p in PIECES[which]:
            p(e, Tile(f, 0, 0))
        with e.Fori(0, B // 2) as i:
            for k in range(2):
                nxt = Tile(f, i, k + 1)

                def hooks(m):
                    for at, p in PIECES[which]:
                        if at == m:
                            p(e, nxt)

                TILES[which](e, Tile(f, i, k), hooks)

    return run, credits


def attention_phase(sb, psum, sem, held, X, ident, w):
    CREDIT = 80
    NT = HEADS * S
    NQ = GROUPS * S
    ln = LayerNorm("att_ln", sb, sem, held)
    xn = sb("att_xn", [P, BLK])
    xh = sb("att_xT_hi", [P, T], F32R)
    xl = sb("att_xT_lo", [P, T], F32R)
    qf = sb("qk_full", [P, 2, T])
    qh = sb("qk_hi", [P, 2, T], F32R)
    qk = sb("qk_parts", [P, 2, GROUPS, T], F32R)
    V = sb("v_padded", [P, S, GROUPS, 4, 32])
    bias = sb("alibi", [P, HEADS, T])
    pn = w["probs"]
    nm = sb("neg_max", [P, NT])
    rs = sb("row_sum", [P, NT])
    ri = sb("row_sum_inv", [P, NT])
    PT = sb("probs_T", [P, 2, 4, T])
    rx = qf[:, 0, :].rearrange("p (q g d) -> p q g d", q=S, g=4)
    rr = qf[:, 1, :]
    yn = sb("att_out_T", [P, GROUPS, T])
    res = xn
    SB = [psum(f"score{j}", [P, T]) for j in range(3)]
    TB = [psum(f"probs_t{j}", [P, T]) for j in range(2)]
    Y = [psum(f"att_y{j}", [P, T]) for j in range(2)]
    M = psum("att_pre_ps", [P, T])
    pre_pe, proj_done, score_done, tr_done, pv_done, rtr_done, out_done = (sem(n) for n in (
        "att_pre_pe", "qk_done", "score_done", "tr_done", "pv_done", "rtr_done", "out_done"))
    x_hi, qf_done, qh_done, exp_done, evac_act, rr_done = (sem(n) for n in (
        "att_x_hi", "qf_done", "qh_done", "att_exp", "evac_act", "rr_done"))
    x_lo, parts_done, v_done, max_done, evac_dve, ri_done, rx_done, yn_done, res_done = (sem(n) for n in (
        "att_x_lo", "parts_done", "v_done", "max_done", "evac_dve", "ri_done", "rx_done", "yn_done", "res_done"))
    setup = sem("att_setup")
    xadd = sem("att_xadd")
    OFF = [384 - P * b for b in range(S)]

    def wait(e, s, v):
        e.wait_ge(s, v + CREDIT)

    def pe_batch(e, b):
        e.wait_ge(ln.dve_done, b * LayerNorm.NDVE + 16)
        wait(e, res_done, b)
        for s in range(S):
            m = e.transpose(M[:, s * P:(s + 1) * P], xn[:, s * D:(s + 1) * D], ident[:])
        m.then_inc(pre_pe, 1)
        wait(e, x_lo, b + 1)
        for n in range(2 * GROUPS):
            bank = SB[n % 2]
            wait(e, qf_done, b * 8 + n - 1)
            wgt = w["qkh"][:, n % 2, n // 2, :], w["qkl"][:, n % 2, n // 2, :]
            e.matmul(bank[:], wgt[0], xh[:], start=True, stop=False)
            e.matmul(bank[:], wgt[1], xh[:], start=False, stop=False)
            e.matmul(bank[:], wgt[0], xl[:], start=False, stop=True).then_inc(proj_done, 1)
        for s in range(S):
            sub = slice(s * P, (s + 1) * P)
            e.matmul(M[:, sub], xh[:, sub], w["vh"][:], start=True, stop=False)
            e.matmul(M[:, sub], xl[:, sub], w["vh"][:], start=False, stop=False)
            m = e.matmul(M[:, sub], xh[:, sub], w["vl"][:], start=False, stop=True)
        m.then_inc(pre_pe, 1)

        def score(t):
            g, qb, G = t % 4, t // 4 % S, t // 16
            if t == 0:
                wait(e, parts_done, b * 8 + 8)
            wait(e, max_done, b * NT + t - 2)
            rows = slice(32 * g, 32 * g + 32)
            e.matmul(SB[t % 3][:, 0:P * (qb + 1)], qk[rows, 0, G, qb * P:(qb + 1) * P],
                     qk[rows, 1, G, 0:P * (qb + 1)], start=True, stop=True).then_inc(score_done, 1)

        def transposes(t):
            qb = t // 4 % S
            wait(e, exp_done, b * NT + t + 1)
            wait(e, evac_act if t % 2 == 0 else evac_dve, b * NT // 2 + t // 2)
            for kb in range(qb + 1):
                m = e.transpose(TB[t % 2][:, kb * P:(kb + 1) * P], pn[:, t % 4, kb * P:(kb + 1) * P], ident[:])
            m.then_inc(tr_done, 1)

        def pv(n):
            G, qb = n // S, n % S
            wait(e, evac_act, b * NT // 2 + 2 * n + 2)
            wait(e, evac_dve, b * NT // 2 + 2 * n + 2)
            if n == 0:
                wait(e, v_done, b + 1)
            if qb == 0:
                wait(e, yn_done, b * GROUPS + G - 1)
            for kb in range(qb + 1):
                for g in range(4):
                    m = e.matmul(Y[G % 2][32 * g:32 * g + 32, qb * P:(qb + 1) * P], V[:, kb, G, g, :],
                                 PT[:, n % 2, g, kb * P:(kb + 1) * P], start=(kb == 0), stop=(kb == qb))
            m.then_inc(pv_done, 1)

        def norm(G):
            wait(e, rx_done, b * GROUPS + G + 1)
            wait(e, rr_done, b * GROUPS + G)
            if G == 0:
                wait(e, v_done, b + 1)
            for qb in range(S):
                m = e.transpose(M[:, qb * P:(qb + 1) * P], rx[:, qb].rearrange("p g d -> p (g d)"), ident[:])
            m.then_inc(rtr_done, 1)

        score(0)
        score(1)
        for t in range(NT):
            if t + 2 < NT:
                score(t + 2)
            transposes(t)
            if t % 4 == 1 and t > 4:
                pv(t // 4 - 1)
            if t % 16 == 3 and t > 16:
                norm(t // 16 - 1)
        pv(NQ - 1)
        norm(GROUPS - 1)
        wait(e, yn_done, b * GROUPS + GROUPS)
        wait(e, rr_done, b * GROUPS + GROUPS)
        for s in range(S):
            for G in range(GROUPS):
                m = e.matmul(M[:, s * D:(s + 1) * D], yn[:, G, s * P:(s + 1) * P], w["wp"][:, G, :],
                             start=(G == 0), stop=(G == GROUPS - 1))
        m.then_inc(out_done, 1)

    def act_batch(e, b):
        ln.act(e, b)
        wait(e, pre_pe, 2 * b + 1)
        e.activation(xh[:], M[:], ACT.Copy).then_inc(x_hi, 1)
        for n in range(2 * GROUPS):
            wait(e, proj_done, b * 8 + n + 1)
            wait(e, parts_done, b * 8 + n - 1)
            bq, scale = (w["bqs"], DH ** -0.5) if n % 2 == 0 else (w["bk"], 1.0)
            e.activation(qf[:, n % 2, :], SB[n % 2][:], ACT.Identity, bias=bq[:, n // 2:n // 2 + 1], scale=scale)\
                .then_inc(qf_done, 1)
            wait(e, qf_done, b * 8 + n + 1)
            e.activation(qh[:, n % 2, :], qf[:, n % 2, :], ACT.Copy).then_inc(qh_done, 1)

        def exp(t):
            wait(e, max_done, b * NT + t + 1)
            p = pn[:, t % 4, 0:P * (t // 4 % S + 1)]
            e.activation(p, p, ACT.Exp, bias=nm[:, t:t + 1], scale=-1.0, accum_out=rs[:, t:t + 1]).then_inc(exp_done, 1)

        def evac(t):
            qb, n = t // 4 % S, t // 4
            wait(e, tr_done, b * NT + t + 1)
            wait(e, pv_done, b * NQ + n - 1)
            e.activation(PT[:, n % 2, t % 4, 0:P * (qb + 1)], TB[t % 2][:, 0:P * (qb + 1)], ACT.Copy)\
                .then_inc(evac_act, 1)

        def rows(G):
            wait(e, rtr_done, b * GROUPS + G + 1)
            wait(e, yn_done, b * GROUPS + G)
            e.activation(rr, M[:], ACT.Copy).then_inc(rr_done, 1)

        for t in range(NT):
            exp(t)
            if t % 2 == 1:
                evac(t - 1)
            if t % 16 == 5 and t > 16:
                rows(t // 16 - 1)
        rows(GROUPS - 1)

    def dve_batch(e, b):
        src = lambda s: X[:, bass.ds(b * BLK + s * D, D)]
        ln.stats(e, b, src)
        ln.apply(e, b, src, lambda s: xn[:, s * D:(s + 1) * D])
        wait(e, x_hi, b + 1)
        e.tensor_tensor(xl[:], M[:], f32(xh[:]), ALU.subtract).then_inc(x_lo, 1)
        for n in range(2 * GROUPS):
            wait(e, qh_done, b * 8 + n + 1)
            e.scalar_tensor_tensor(qk[:, n % 2, n // 2, :], f32(qh[:, n % 2, :]), w["minus_lo"][:, n % 2:n % 2 + 1],
                                   qf[:, n % 2, :], ALU.mult, ALU.add).then_inc(parts_done, 1)
        wait(e, pre_pe, 2 * b + 2)
        e.tensor_tensor(V[:, :, :, :, 0:DH].rearrange("p s a g d -> p s (a g) d"),
                        M[:].rearrange("p (s n d) -> p s n d", s=S, d=DH),
                        w["bv"][:].rearrange("p (o n d) -> p o n d", o=1, d=DH).to_broadcast([P, S, HEADS, DH]),
                        ALU.add).then_inc(v_done, 1)

        def maxima(t):
            qb, hd = t // 4 % S, 4 * (t // 16) + t % 4
            wait(e, score_done, b * NT + t + 1)
            hold(e, tr_done, b * NT + t - 3 + CREDIT, held)
            width = P * (qb + 1)
            e.tensor_tensor_reduce(pn[:, t % 4, 0:width], SB[t % 3][:, 0:width], bias[:, hd, OFF[qb]:T],
                                   -1.0, 3.0e38, ALU.add, ALU.min, nm[:, t:t + 1]).then_inc(max_done, 1)

        def evac(t):
            qb, n = t // 4 % S, t // 4
            wait(e, tr_done, b * NT + t + 1)
            wait(e, pv_done, b * NQ + n - 1)
            e.tensor_copy(PT[:, n % 2, t % 4, 0:P * (qb + 1)], TB[t % 2][:, 0:P * (qb + 1)]).then_inc(evac_dve, 1)

        def inverse(G):
            wait(e, exp_done, b * NT + 16 * G + 16)
            e.reciprocal(ri[:, 16 * G:16 * G + 16], rs[:, 16 * G:16 * G + 16]).then_inc(ri_done, 1)
            wait(e, ri_done, b * GROUPS + G + 1)
            wait(e, rtr_done, b * GROUPS + G)
            e.tensor_copy(rx, ri[:, 16 * G:16 * G + 16].rearrange("p (q g o) -> p q g o", q=S, o=1)
                          .to_broadcast([P, S, 4, 32])).then_inc(rx_done, 1)

        def normed(G):
            wait(e, rr_done, b * GROUPS + G + 1)
            wait(e, pv_done, b * NQ + S * G + S)
            e.tensor_tensor(yn[:, G, :], Y[G % 2][:], rr, ALU.mult).then_inc(yn_done, 1)

        for t in range(NT):
            maxima(t)
            if t >= 3 and t % 2 == 1:
                evac(t - 2)
            if t % 16 == 1 and t > 16:
                inverse(t // 16 - 1)
            if t % 16 == 7 and t > 16:
                normed(t // 16 - 1)
        evac(NT - 1)
        inverse(GROUPS - 1)
        normed(GROUPS - 1)
        wait(e, out_done, b + 1)
        e.tensor_tensor(res[:].rearrange("p (s d) -> p s d", s=S), M[:].rearrange("p (s d) -> p s d", s=S),
                        w["bp"][:].rearrange("p (o d) -> p o d", o=1).to_broadcast([P, S, D]), ALU.add)\
            .then_inc(res_done, 1)
        wait(e, res_done, b + 1)
        xb = X[:, bass.ds(b * BLK, BLK)]
        e.tensor_tensor(xb, xb, res[:], ALU.add).then_inc(xadd, 1)

    OWN = {"pe": (pre_pe, proj_done, score_done, tr_done, pv_done, rtr_done, out_done),
           "act": (x_hi, qf_done, qh_done, exp_done, evac_act, rr_done),
           "dve": (x_lo, parts_done, v_done, max_done, evac_dve, ri_done, rx_done, yn_done, res_done), "pool": ()}
    BATCH = {"pe": pe_batch, "act": act_batch, "dve": dve_batch}

    def dve_setup(e):
        for s in OWN["dve"]:
            e.sem_inc(s, CREDIT)
        ln.setup(e).then_inc(setup, 1)
        e.memset(V[:], 0.0).then_inc(setup, 1)
        e.tensor_scalar(w["bqs"][:], w["bq"][:], DH ** -0.5, None, ALU.mult).then_inc(setup, 1)
        for hd in range(HEADS):
            e.scalar_tensor_tensor(bias[:, hd, :], w["rel"], w["slopes"][:, hd:hd + 1], w["mask"],
                                   ALU.mult, ALU.add).then_inc(setup, 1)

    def run(e, which):
        if which == "dve":
            dve_setup(e)
        else:
            for s in OWN[which]:
                e.sem_inc(s, CREDIT)
        e.wait_ge(setup, 3 + HEADS)
        if which == "pool":
            return
        with e.Fori(0, B) as b:
            BATCH[which](e, b)

    return run


def build(nc, x, win, cw, cb, xp, dtw, dtb, alog, dskip, wout, lnw, lnb, wqk, bqk, wv, bv, wp, bp, slopes,
          ws, bs, wffn, id_dram, rel, mask, minus_lo, iota, out):
    with ExitStack() as ctx:
        def allocators(c):
            return (lambda name, shape, dt=F32: c.enter_context(nc.sbuf_tensor(name, shape, dt)),
                    lambda name, shape, dt=F32: c.enter_context(nc.psum_tensor(name, shape, dt)))

        def sem(name):
            return ctx.enter_context(nc.semaphore(name))

        def row(a):
            n = a.shape[0]
            return a.rearrange("(o n) -> o n", o=1).to_broadcast([P, n])

        sb, psum = allocators(ctx)
        X = sb("stream", [P, (B + 2) * BLK])
        ident = sb("ident", [P, P])
        loaded, stored, phase_end, held = sem("loaded"), sem("stored"), sem("phase_end"), sem("held")
        loads, late = [], []
        with ExitStack() as c1:
            sb1, psum1 = allocators(c1)
            w = {"in": sb1("w_in", [P, L, 2 * DI]), "cw": sb1("w_conv", [P, L, H, KC]), "cb": sb1("b_conv", [P, L, H]),
                 "xp": sb1("w_xp", [P, L, H, 40]), "dt": sb1("w_dt", [64, L, DI]), "dtb": sb1("b_dt", [P, L, H]),
                 "alog": sb1("a_log", [P, L, H, NS]), "D": sb1("d_skip", [P, L, H]), "out": sb1("w_out", [P, L, H, D]),
                 "lnw": sb1("ln_w", [P, L, D]), "lnb": sb1("ln_b", [P, L, D]), "id2": sb1("id2", [64, 32])}
            flat = lambda t: t[:].rearrange("p l d -> p (l d)")
            loads = [(X[:, 0:B * BLK].rearrange("p (n d) -> p n d", d=D), x.rearrange("b (s p) d -> p (b s) d", p=P)),
                     (ident[:], id_dram), (w["in"][:], win), (w["cw"][:], cw), (w["cb"][:], cb), (w["xp"][:], xp),
                     (w["dt"][32:40], dtw), (w["dtb"][:], dtb), (w["alog"][:], alog), (w["D"][:], dskip),
                     (w["out"][:], wout), (flat(w["lnw"]), row(lnw.rearrange("l d -> (l d)"))),
                     (flat(w["lnb"]), row(lnb.rearrange("l d -> (l d)"))),
                     (w["id2"][0:32], id_dram[0:32, 0:32]), (w["id2"][32:64], id_dram[0:32, 0:32])]
            mamba = mamba_phase(sb1, psum1, sem, held, X, w, ident, loaded, len(loads))

        WH, WL = sb("ffn_w_hi", [P, E_, WCOL], F32R), sb("ffn_w_lo", [P, E_, WCOL], F32R)
        sel8 = sb("expert_select", [E_, E_, P], F32R)
        small = {"ws": sb("w_router", [P, E_]), "bs": sb("b_router", [P, E_]), "iota": sb("iota", [P, E_])}

        def ffn_w(t):
            def get(kind, at):
                ex, j, rows = at
                if kind == "down":
                    return t[0:rows, ex, 2 * F_ + j * D:2 * F_ + (j + 1) * D]
                first = (F_ if kind == "up" else 0) + j * P
                return t[:, ex, first:first + rows]
            return get

        with ExitStack() as c2:
            sb2, _ = allocators(c2)
            raw = sb2("raw_weights", [P, 2, WCOL])
            raw_loaded = (sem("raw_loaded0"), sem("raw_loaded1"))
        with ExitStack() as c3:
            sb3, psum3 = allocators(c3)
            ffn, ffn_credits = ffn_phase(sb3, psum3, sem, held, X, ident, ffn_w(WH), ffn_w(WL), small["ws"],
                                                 small["bs"], small["iota"], sel8)
        with ExitStack() as c4:
            sb4, psum4 = allocators(c4)
            probs = sb4("probs", [P, 4, T])
            aw = {"probs": probs, "rel": probs[:, 0, :], "mask": probs[:, 1, :],
                  "raw_qk": probs[:, 2:4, :].rearrange("p a (g m) -> p a g m", g=GROUPS),
                  "qkh": sb4("w_qk_hi", [P, 2, GROUPS, P], F32R),
                  "qkl": sb4("w_qk_lo", [P, 2, GROUPS, P], F32R), "raw_v": sb4("w_v", [P, D]),
                  "vh": sb4("w_v_hi", [P, D], F32R), "vl": sb4("w_v_lo", [P, D], F32R),
                  "wp": sb4("w_proj", [P, GROUPS, D]), "bp": sb4("b_proj", [P, D]), "bv": sb4("b_v", [P, D]),
                  "bq": sb4("b_q", [P, GROUPS]), "bk": sb4("b_k", [P, GROUPS]), "bqs": sb4("b_q_scaled", [P, GROUPS]),
                  "slopes": sb4("slopes", [P, HEADS]),
                  "minus_lo": sb4("minus_lo", [P, 2])}
            att_loads = [(aw["raw_qk"], wqk), (aw["raw_v"][:], wv), (aw["wp"][:], wp), (aw["bp"][:], row(bp)),
                         (aw["bv"][:], row(bv)), (aw["bq"][:], bqk[:, 0, :]), (aw["bk"][:], bqk[:, 1, :]),
                         (aw["slopes"][:], row(slopes)), (aw["rel"], rel), (aw["mask"], mask),
                         (aw["minus_lo"][:], minus_lo)]
            att = attention_phase(sb4, psum4, sem, held, X, ident, aw)
        ffn_loaded, att_loaded = sem("ffn_loaded"), sem("att_loaded")
        split_hi, split_lo, ffn_ready, att_split = (sem(n) for n in ("split_hi", "split_lo", "ffn_ready", "att_split"))
        block = ctx.enter_context(nc.Block())

        @block.sync
        def _(sp):
            for dst, src in loads:
                sp.dma_start(dst, src).then_inc(loaded, 16)
            sp.wait_ge(phase_end, 4)
            for dst, src in ((small["ws"][:], ws), (small["bs"][:], row(bs)), (small["iota"][:], iota)):
                sp.dma_start(dst, src).then_inc(ffn_loaded, 16)
            for ex in range(E_):
                if ex >= 2:
                    sp.wait_ge(split_lo, ex - 1)
                sp.dma_start(raw[:, ex % 2, :], wffn[:, ex, :]).then_inc(raw_loaded[ex % 2], 16)
            sp.wait_ge(phase_end, 12)
            for dst, src in att_loads:
                sp.dma_start(dst, src).then_inc(att_loaded, 16)
            sp.wait_ge(phase_end, 20)
            sp.dma_start(out.rearrange("b (s p) d -> p (b s) d", p=P),
                         X[:, 0:B * BLK].rearrange("p (n d) -> p n d", d=D)).then_inc(stored, 16)
            sp.wait_ge(stored, 16)

        def phases(e, which):
            mamba(e, which)
            barrier(e, phase_end, 1)
            e.wait_ge(ffn_loaded, 48)
            ffn_credits(e, which)
            if which == "act":
                for ex in range(E_):
                    e.wait_ge(raw_loaded[ex % 2], 16 * (ex // 2 + 1))
                    e.activation(WH[:, ex, :], raw[:, ex % 2, :], ACT.Copy).then_inc(split_hi, 1)
            if which == "dve":
                e.tensor_copy(sel8[:], ident[0:E_, 0:E_].rearrange("p (n o) -> p n o", o=1).to_broadcast([E_, E_, P]))\
                    .then_inc(ffn_ready, 1)
                for ex in range(E_):
                    e.wait_ge(split_hi, ex + 1)
                    e.tensor_tensor(WL[:, ex, :], raw[:, ex % 2, :], f32(WH[:, ex, :]), ALU.subtract)\
                        .then_inc(split_lo, 1)
            e.wait_ge(split_lo, E_)
            e.wait_ge(ffn_ready, 1)
            barrier(e, phase_end, 2)
            ffn(e, which, 0)
            barrier(e, phase_end, 3)
            e.wait_ge(att_loaded, 16 * len(att_loads))
            if which == "act":
                e.activation(aw["qkh"][:], aw["raw_qk"], ACT.Copy).then_inc(att_split, 1)
                e.activation(aw["vh"][:], aw["raw_v"][:], ACT.Copy).then_inc(att_split, 1)
            if which == "dve":
                e.wait_ge(att_split, 2)
                e.tensor_tensor(aw["qkl"][:], aw["raw_qk"], f32(aw["qkh"][:]), ALU.subtract).then_inc(att_split, 1)
                e.tensor_tensor(aw["vl"][:], aw["raw_v"][:], f32(aw["vh"][:]), ALU.subtract).then_inc(att_split, 1)
            e.wait_ge(att_split, 4)
            att(e, which)
            barrier(e, phase_end, 4)
            ffn(e, which, 1)
            barrier(e, phase_end, 5)

        @block.tensor
        def _(pe):
            phases(pe, "pe")

        @block.scalar
        def _(act):
            phases(act, "act")

        @block.vector
        def _(dve):
            phases(dve, "dve")

        @block.gpsimd
        def _(pool):
            phases(pool, "pool")


def kernel(**inputs):
    import numpy as np
    import concourse.bacc as bacc
    from concourse.bass_utils import run_bass_kernel_spmd

    m = {k.removeprefix("L0_"): np.asarray(v) for k, v in inputs.items()}
    a = lambda n: m["attn_a_" + n]

    def halves(v):
        return v.reshape(L, H, P, -1).transpose(2, 0, 1, 3)

    x_proj = np.concatenate([a("x_proj_w")[:, R:], a("x_proj_w")[:, :R]], axis=1)
    kqv, bkqv = m["attn_b_W_kqv"], m["attn_b_b_kqv"]

    def stacked(v):
        v = v.reshape(v.shape[0], GROUPS, 4, 1, DH)
        return np.broadcast_to(v, (v.shape[0], GROUPS, 4, 4, DH)).reshape(v.shape[0], GROUPS, P)

    wd = np.zeros((E_, 3 * P, D), np.float32)
    wd[:, :F_] = m["ffn_Wd"]
    wffn = np.concatenate([m["ffn_Wg"].transpose(1, 0, 2), m["ffn_Wu"].transpose(1, 0, 2),
                           wd.reshape(E_, 3, P, D).transpose(2, 0, 1, 3).reshape(P, E_, 3 * D)], axis=2)
    wp = np.zeros((GROUPS, 4, 32, D), np.float32)
    wp[:, :, :DH] = m["attn_b_W_proj"].reshape(GROUPS, 4, DH, D)
    col, part = np.arange(T) - 3 * P, np.arange(P)[:, None]
    copy = np.arange(P) // DH % 4
    arrays = {
        "x": a("x"), "win": a("in_proj_w").transpose(2, 0, 1), "cw": halves(a("conv_w")),
        "cb": halves(a("conv_b"))[..., 0], "xp": x_proj.transpose(0, 2, 1).reshape(L, H, P, 40).transpose(2, 0, 1, 3),
        "dtw": a("dt_proj_w").transpose(2, 0, 1), "dtb": halves(a("dt_proj_b"))[..., 0], "alog": halves(a("A_log")),
        "dskip": halves(a("Dskip"))[..., 0],
        "wout": a("out_proj_w").transpose(0, 2, 1).reshape(L, H, P, D).transpose(2, 0, 1, 3),
        "lnw": a("ln_w"), "lnb": a("ln_b"),
        "wqk": np.stack([stacked(kqv[:, D:2 * D]), stacked(kqv[:, 0:D])], axis=1),
        "bqk": np.stack([stacked(bkqv[None, D:2 * D])[0], stacked(bkqv[None, 0:D])[0]]).transpose(2, 0, 1),
        "wv": kqv[:, 2 * D:], "bv": bkqv[2 * D:], "wp": wp.reshape(GROUPS, P, D).transpose(1, 0, 2),
        "bp": m["attn_b_b_proj"], "slopes": m["attn_b_slopes"],
        "ws": m["ffn_Ws"], "bs": m["ffn_bs"], "wffn": wffn,
        "ident": np.eye(P, dtype=np.float32),
        "rel": (col - part).astype(np.float32), "mask": np.where(col > part, np.float32(NEG), np.float32(0)),
        "minus_lo": -np.stack([copy % 2, copy // 2], axis=1).astype(np.float32),
        "iota": np.broadcast_to(np.arange(E_, dtype=np.float32), (P, E_)),
    }
    arrays = {k: np.ascontiguousarray(v) for k, v in arrays.items()}
    nc = bacc.Bacc("TRN2", target_bir_lowering=False, num_devices=1)
    args = [nc.dram_tensor("in_" + k, v.shape, F32, kind="ExternalInput").ap() for k, v in arrays.items()]
    args.append(nc.dram_tensor("out_x", (B, T, D), F32, kind="ExternalOutput").ap())
    build(nc, *args)
    r = run_bass_kernel_spmd(nc, [{"in_" + k: v for k, v in arrays.items()}], core_ids=[0])
    return r.results[0]["out_x"]
```

```python
from contextlib import ExitStack

import concourse.bass as bass
from concourse import mybir
from concourse.alu_op_type import AluOpType as ALU

F32 = mybir.dt.float32
F32R = mybir.dt.float32r
U32 = mybir.dt.uint32
ACT = mybir.ActivationFunctionType
AX = mybir.AxisListType
EPS = 1e-5

B, T, D = 8, 512, 128
P = 128
S = T // P
L = 2
DI, H = 256, 2
NS, R, KC = 16, 8, 4
QUAD = 4
UNITS = QUAD * L
BLK = S * D


def hold(e, s, v, held):
    e.wait_ge(s, v)
    e.sem_inc(held, 1)


class LayerNorm:
    NDVE, NACT = 16, 2

    def __init__(self, name, sb, sem, held, base=0):
        self.held = held
        self.base = base
        self.st = sb(name + "_bn", [P, S, 6])
        self.mv = sb(name + "_mean_var", [P, S, 2])
        self.r = sb(name + "_rstd", [P, 4, S])
        self.eps = sb(name + "_eps", [P, 1])
        self.dve_done, self.act_done = sem(name + "_dve"), sem(name + "_act")

    def setup(self, e):
        return e.memset(self.eps[:], EPS)

    def stats(self, e, v, src):
        for s in range(S):
            e.bn_stats(self.st[:, s, :], src(s)).then_inc(self.dve_done, 1)
        for s in range(S):
            hold(e, self.dve_done, v * self.NDVE + self.base + (1 + s), self.held)
            e.bn_aggr(self.mv[:, s, :], self.st[:, s, :]).then_inc(self.dve_done, 1)

    def act(self, e, v):
        e.wait_ge(self.dve_done, v * self.NDVE + self.base + 8)
        e.activation(self.r[:, 0, :], self.mv[:, :, 1], ACT.Ln, bias=self.eps[:, 0:1]).then_inc(self.act_done, 1)
        e.wait_ge(self.act_done, v * self.NACT + 1)
        e.activation(self.r[:, 1, :], self.r[:, 0, :], ACT.Exp, scale=-0.5).then_inc(self.act_done, 1)

    def apply(self, e, v, src, dst):
        r, r2, t = self.r[:, 1, :], self.r[:, 2, :], self.r[:, 3, :]
        at = lambda n: e.wait_ge(self.dve_done, v * self.NDVE + self.base + n)
        e.wait_ge(self.act_done, v * self.NACT + 2)
        e.tensor_tensor(r2, r, r, ALU.mult).then_inc(self.dve_done, 1)
        at(9)
        e.scalar_tensor_tensor(t, self.mv[:, :, 1], EPS, r2, ALU.add, ALU.mult).then_inc(self.dve_done, 1)
        at(10)
        e.tensor_scalar(t, t, -0.5, 1.5, ALU.mult, ALU.add).then_inc(self.dve_done, 1)
        at(11)
        e.tensor_tensor(r2, r, t, ALU.mult).then_inc(self.dve_done, 1)
        at(12)
        for s in range(S):
            e.tensor_scalar(dst(s), src(s), self.mv[:, s, 0:1], r2[:, s:s + 1], ALU.subtract, ALU.mult)\
                .then_inc(self.dve_done, 1)


def mamba_phase(sb, psum, sem, held, X, w, ident, loaded, loads):
    RING = 4
    a = sb("decay", [P, RING, H * T])
    g = sb("drive", [P, RING, H * T])
    h = sb("state", [P, RING, H * T])
    hc = sb("state_c", [P, 2, H * T])
    bsb = sb("b_rows", [P, RING, T])
    u = sb("u", [P, 2, H * T])
    sz = sb("silu_z", [P, 2, H * T])
    dt = sb("dt", [P, 2, H * T])
    dtu = sb("dtu", [P, 2, H * T])
    xcp = sb("xc_padded", [P, H, KC - 1 + T])
    cv = sb("conv", [P, H * T])
    t1 = sb("t1", [P, H * T])
    t2 = sb("t2", [P, H * T])
    t3 = sb("t3", [P, H * T])
    yg = sb("y_gated", [P, H * T])
    xT = sb("xT", [P, T])
    bc = sb("bc_split", [64, 2, T], F32R)
    dtr = sb("dt_low_rank", [64, T])
    zs = sb("z_stage", [P, QUAD, S * D])
    hn = sb("normed", [P, S * D])
    sel = sb("row_select", [64, 2 * NS, P], F32R)
    Aneg = sb("a_neg", [P, L, H, NS])

    PB = [psum(f"rep_b{j}", [P, T]) for j in range(2)]
    PC = [psum(f"rep_c{j}", [P, T]) for j in range(2)]
    Y = [psum(f"y{j}", [P, T]) for j in range(H)]
    S0, S1 = psum("s0", [P, T]), psum("s1", [P, T])

    CREDIT = 40
    rep_b_done = sem("rep_b_done")
    rep_c_done = sem("rep_c_done")
    bcopy_done = sem("bcopy_done")
    exp_done = sem("exp_done")
    drive_done = sem("drive_done")
    scan_done = sem("scan_done")
    cmul_done = sem("cmul_done")
    nsum_done = sem("nsum_done")
    pre_pe, pre_act, pre_dve, pre_pool = sem("pre_pe"), sem("pre_act"), sem("pre_dve"), sem("pre_pool")
    post_pe, post_act, post_dve, post_pool = sem("post_pe"), sem("post_act"), sem("post_dve"), sem("post_pool")
    setup = sem("mamba_setup")
    ln_in = LayerNorm("ln_in", sb, sem, held)
    ln_out = LayerNorm("ln_out", sb, sem, held, CREDIT)
    NPE, NACT, NDVE = 8, 16, 8
    QPE, QDVE = 1, 3
    POST_POOL = [0, 3, 6, 9, 12, 16, 20, 24]
    QPOOL = 28

    class At:
        def __init__(self, i, k):
            self.i, self.k, self.q, self.l = i, k % UNITS, k % 2, (k % UNITS) // QUAD
            self.z = k % QUAD

        def step(self, n, per=1):
            return self.i * (UNITS * NS * per) + (self.k * NS * per + n * per)

        def count(self, per, n):
            return self.i * (UNITS * per) + (self.k * per + n)

    def wait(e, s, v):
        e.wait_ge(s, v + CREDIT)

    def wait_post_norm(e, c):
        back = 2 if c.k == 1 else 3
        e.wait_ge(ln_out.dve_done, c.count(LayerNorm.NDVE, (1 - back) * LayerNorm.NDVE) + CREDIT)

    def pe_tr(e, c):
        if c.l == 0:
            e.wait_ge(ln_in.dve_done, (c.i * QUAD + c.z) * LayerNorm.NDVE + 16)
        else:
            wait(e, post_pool, c.i * QPOOL + 3 * (c.z + 1))
        wait(e, pre_act, c.count(NACT, -NACT + 12))
        for s in range(S):
            m = e.transpose(S0[:, s * P:(s + 1) * P], zs[:, c.z, s * D:(s + 1) * D], ident[:])
        m.then_inc(pre_pe, 1)

    def pe_inproj(e, c, j):
        out = S1 if j % 2 == 0 else S0
        if j == 0:
            wait(e, pre_act, c.count(NACT, 1))
            wait_post_norm(e, c)
        elif j > 1:
            wait(e, pre_act, c.count(NACT, j))
        e.matmul(out[:], w["in"][:, c.l, j * P:(j + 1) * P], xT[:], start=True, stop=True).then_inc(pre_pe, 1)

    def pe_xproj(e, c):
        wait(e, pre_act, c.count(NACT, 8))
        for hh in range(H):
            m = e.matmul(S1[0:40, :], w["xp"][:, c.l, hh, :], u[:, c.q, hh * T:(hh + 1) * T],
                         start=(hh == 0), stop=(hh == H - 1))
        m.then_inc(pre_pe, 1)

    def pe_dtproj(e, c):
        wait(e, pre_act, c.count(NACT, 10))
        for hh in range(H):
            if hh == 1:
                wait(e, pre_dve, c.count(NDVE, 7))
            e.matmul((S0, S1)[hh][:], w["dt"][32:40, c.l, hh * P:(hh + 1) * P], dtr[32:40, :],
                     start=True, stop=True).then_inc(pre_pe, 1)

    def pe_out(e, c, latest):
        wait(e, pre_act, latest.count(NACT, 14))
        wait(e, post_dve, c.count(QDVE, 3))
        for s in range(S):
            for hh in range(H):
                m = e.matmul(S1[:, s * D:(s + 1) * D], yg[:, hh * T + s * P:hh * T + (s + 1) * P],
                             w["out"][:, c.l, hh, :], start=(hh == 0), stop=(hh == H - 1))
        m.then_inc(post_pe, 1)

    def nsum(e, c, n):
        wait(e, cmul_done, c.step(n + 1))
        if n == 0:
            wait(e, post_dve, c.count(QDVE, -QDVE + 2))
        for hh in range(H):
            m = e.matmul(Y[hh][:], ident[:], hc[:, n % 2, hh * T:(hh + 1) * T],
                         start=(n == 0), stop=(n == NS - 1))
        m.then_inc(nsum_done, 1)

    def rep_b(e, c, n):
        if n == 0:
            wait(e, pre_dve, c.count(NDVE, 7))
        wait(e, bcopy_done, c.step(n - 1))
        e.matmul(PB[n % 2][:], sel[:, n, :], bc[:, c.q, :], start=True, stop=True).then_inc(rep_b_done, 1)

    def rep_c(e, c, n):
        wait(e, cmul_done, c.step(n - 1))
        e.matmul(PC[n % 2][:], sel[:, NS + n, :], bc[:, c.q, :], start=True, stop=True).then_inc(rep_c_done, 1)

    def pe_begin(e, c):
        for n in range(3):
            rep_b(e, c, n)
        rep_c(e, c, 0)

    def pe_steps(e, before, c, nxt, hooks):
        for n in range(NS):
            rep_b(e, *step_of(c, nxt, n + 3))
            rep_c(e, *step_of(c, nxt, n + 1))
            if n >= 1:
                nsum(e, c, n - 1)
            elif before is not None:
                nsum(e, before, NS - 1)
            hooks(n)

    def act_pre_a(e, c):
        wait(e, pre_pe, c.count(NPE, 1))
        e.activation(xT[:], S0[:], ACT.Copy).then_inc(pre_act, 1)

    def act_pre_xc(e, c):
        for hh in range(H):
            wait(e, pre_pe, c.count(NPE, 2 + hh))
            e.activation(xcp[:, hh, KC - 1:], (S1, S0)[hh][:], ACT.Copy).then_inc(pre_act, 1)
        wait(e, pre_act, c.count(NACT, 3))
        for hh in range(H):
            e.activation(cv[:, hh * T:(hh + 1) * T], xcp[:, hh, 0:T], ACT.Identity,
                         bias=w["cb"][:, c.l, hh:hh + 1], scale=w["cw"][:, c.l, hh, 0:1]).then_inc(pre_act, 1)

    def act_pre_b(e, c):
        wait(e, post_dve, c.count(QDVE, -2 * QDVE + 3))
        for hh in range(H):
            wait(e, pre_pe, c.count(NPE, 4 + hh))
            e.activation(sz[:, c.q, hh * T:(hh + 1) * T], (S1, S0)[hh][:], ACT.Silu).then_inc(pre_act, 1)
        wait(e, pre_dve, c.count(NDVE, 6))
        e.activation(u[:, c.q, :], cv[:], ACT.Silu).then_inc(pre_act, 1)
        e.preload_act_table_set("natural_log_exp_and_others")

    def act_pre_c(e, c):
        wait(e, pre_pe, c.count(NPE, 6))
        e.activation(bc[0:32, c.q, :], S1[0:32, :], ACT.Copy).then_inc(pre_act, 1)
        e.activation(dtr[32:40, :], S1[32:40, :], ACT.Copy).then_inc(pre_act, 1)

    def act_pre_d(e, c):
        for hh in range(H):
            part = slice(hh * T, (hh + 1) * T)
            wait(e, pre_pe, c.count(NPE, 7 + hh))
            e.activation(t1[:, part], (S0, S1)[hh][:], ACT.Abs, bias=w["dtb"][:, c.l, hh:hh + 1]).then_inc(pre_act, 1)
            e.activation(t3[:, part], (S0, S1)[hh][:], ACT.Relu, bias=w["dtb"][:, c.l, hh:hh + 1]).then_inc(pre_act, 1)

    def act_pre_e(e, c):
        wait(e, pre_act, c.count(NACT, 13))
        e.activation(t2[:], t1[:], ACT.Exp, scale=-1.0).then_inc(pre_act, 1)
        wait(e, pre_act, c.count(NACT, 15))
        e.activation(t1[:], t2[:], ACT.Ln, bias=1.0).then_inc(pre_act, 1)

    def act_ln_in(e, c):
        ln_in.act(e, c.i * QUAD + c.z)

    def act_post(e, c):
        ln_out.act(e, c.unit)

    def copy_b(e, c, n):
        wait(e, rep_b_done, c.step(n + 1))
        wait(e, drive_done, c.step(n - RING + 1))
        e.activation(bsb[:, n % RING, :], PB[n % 2][:], ACT.Copy).then_inc(bcopy_done, 1)

    def act_begin(e, c):
        copy_b(e, c, 0)

    def act_steps(e, before, c, nxt, hooks):
        for n in range(NS):
            copy_b(e, *step_of(c, nxt, n + 1))
            if n == 0:
                wait(e, pre_dve, c.count(NDVE, 8))
            wait(e, scan_done, c.step(n - RING + 1))
            for hh in range(H):
                m = e.activation(a[:, n % RING, hh * T + 1:(hh + 1) * T], dt[:, c.q, hh * T + 1:(hh + 1) * T],
                                 ACT.Exp, scale=Aneg[:, c.l, hh, n:n + 1])
            m.then_inc(exp_done, 1)
            hooks(n)

    def two(ap):
        return ap.rearrange("p (o t) -> p o t", o=1).to_broadcast([P, H, T])

    def halves(ap):
        return ap.rearrange("p (h t) -> p h t", h=H)

    def pool_steps(e, before, c, nxt, hooks):
        for n in range(NS):
            if n == 0:
                wait(e, pre_pool, c.count(1, 1))
            wait(e, bcopy_done, c.step(n + 1))
            wait(e, scan_done, c.step(n - RING + 1))
            e.tensor_tensor(halves(g[:, n % RING, :]), halves(dtu[:, c.q, :]), two(bsb[:, n % RING, :]),
                            ALU.mult).then_inc(drive_done, 1)
            hooks(n)

    def pool_dtu(e, c):
        wait(e, pre_dve, c.count(NDVE, 8))
        e.tensor_tensor(dtu[:, c.q, :], dt[:, c.q, :], u[:, c.q, :], ALU.mult).then_inc(pre_pool, 1)

    def rows_of(ap):
        return ap.rearrange("p (s d) -> p s d", s=S)

    def over(ap):
        return ap.rearrange("p (o d) -> p o d", o=1).to_broadcast([P, S, D])

    def pool_post_a(e, c):
        e.wait_ge(ln_out.dve_done, c.unit * LayerNorm.NDVE + 16 + CREDIT)
        e.tensor_tensor(rows_of(hn[:]), rows_of(hn[:]), over(w["lnw"][:, c.l, :]), ALU.mult).then_inc(post_pool, 1)

    def pool_post_b(e, c):
        wait(e, post_pool, c.i * QPOOL + POST_POOL[c.k] + 1)
        e.tensor_tensor(rows_of(hn[:]), rows_of(hn[:]), over(w["lnb"][:, c.l, :]), ALU.add).then_inc(post_pool, 1)

    def pool_post_c(e, c):
        wait(e, post_pool, c.i * QPOOL + POST_POOL[c.k] + 2)
        if c.l == 0:
            e.tensor_tensor(zs[:, c.z, :], zs[:, c.z, :], hn[:], ALU.add).then_inc(post_pool, 1)
        else:
            e.tensor_tensor(hn[:], zs[:, c.z, :], hn[:], ALU.add).then_inc(post_pool, 1)
            wait(e, post_pool, c.i * QPOOL + POST_POOL[c.k] + 3)
            xb = X[:, bass.ds(c.batch * BLK, BLK)]
            e.tensor_tensor(xb, xb, hn[:], ALU.add).then_inc(post_pool, 1)

    def dve_conv(e, c, k):
        for hh in range(H):
            part = slice(hh * T, (hh + 1) * T)
            if k == 1:
                wait(e, pre_act, c.count(NACT, 4 + hh))
            else:
                wait(e, pre_dve, c.count(NDVE, 2 * (k - 2) + hh + 1))
            e.scalar_tensor_tensor(cv[:, part], xcp[:, hh, k:k + T], w["cw"][:, c.l, hh, k:k + 1], cv[:, part],
                                   ALU.mult, ALU.add).then_inc(pre_dve, 1)

    def dve_bc(e, c):
        wait(e, pre_act, c.count(NACT, 9))
        e.tensor_tensor(bc[32:64, c.q, :], S1[0:32, :], bc[0:32, c.q, :].bitcast(F32), ALU.subtract)\
            .then_inc(pre_dve, 1)

    def dve_dt(e, c):
        wait(e, pre_act, c.count(NACT, 16))
        e.tensor_tensor(dt[:, c.q, :], t1[:], t3[:], ALU.add).then_inc(pre_dve, 1)

    def dve_post_a(e, c):
        wait(e, nsum_done, c.step(NS))
        for hh in range(H):
            part = slice(hh * T, (hh + 1) * T)
            e.scalar_tensor_tensor(yg[:, part], u[:, c.q, part], w["D"][:, c.l, hh:hh + 1], Y[hh][:],
                                   ALU.mult, ALU.add).then_inc(post_dve, 1)
        wait(e, post_dve, c.count(QDVE, 2))
        e.tensor_tensor(yg[:], yg[:], sz[:, c.q, :], ALU.mult).then_inc(post_dve, 1)

    def dve_post_b(e, c):
        wait(e, post_pe, c.count(QPE, 1))
        ln_out.stats(e, c.unit, lambda s: S1[:, s * D:(s + 1) * D])

    def dve_post_c(e, c):
        wait(e, post_pool, c.i * QPOOL + POST_POOL[c.k])
        ln_out.apply(e, c.unit, lambda s: S1[:, s * D:(s + 1) * D], lambda s: hn[:, s * D:(s + 1) * D])

    def x_block(c, s):
        return X[:, bass.ds(c.batch * BLK + s * D, D)]

    def dve_ln_in_a(e, c):
        ln_in.stats(e, c.i * QUAD + c.z, lambda s: x_block(c, s))

    def dve_ln_in_b(e, c):
        wait(e, post_pool, (c.i - 1) * QPOOL + POST_POOL[QUAD] + 4 * (c.z + 1))
        ln_in.apply(e, c.i * QUAD + c.z, lambda s: x_block(c, s), lambda s: zs[:, c.z, s * D:(s + 1) * D])

    def cmul(e, c, n):
        wait(e, rep_c_done, c.step(n + 1))
        wait(e, scan_done, c.step(n + 1))
        wait(e, nsum_done, c.step(n - 1))
        e.tensor_tensor(halves(hc[:, n % 2, :]), halves(h[:, n % RING, :]), two(PC[n % 2][:]),
                        ALU.mult).then_inc(cmul_done, 1)

    def dve_steps(e, before, c, nxt, hooks):
        for n in range(NS):
            if n >= 1:
                cmul(e, c, n - 1)
            elif before is not None:
                cmul(e, before, NS - 1)
            wait(e, exp_done, c.step(n + 1))
            wait(e, drive_done, c.step(n + 1))
            wait(e, cmul_done, c.step(n - RING + 1))
            e.tensor_tensor_scan(h[:, n % RING, :], a[:, n % RING, :], g[:, n % RING, :], 0.0, ALU.mult, ALU.add)\
                .then_inc(scan_done, 1)
            hooks(n)

    def arg(f, j):
        return lambda e, c: f(e, c, j)

    PIECES = {
        "pe": [(0, "pre", pe_tr), (3, "pre", arg(pe_inproj, 0)), (3, "pre", arg(pe_inproj, 1)),
               (5, "pre", arg(pe_inproj, 2)), (6, "pre", arg(pe_inproj, 3)), (7, "pre", pe_xproj),
               (10, "pre", pe_dtproj), (11, "post", pe_out)],
        "act": [(2, "pre", act_pre_a), (5, "pre", act_pre_xc), (8, "pre", act_pre_b), (11, "pre", act_pre_c),
                (12, "pre", act_pre_d), (13, "pre", act_pre_e), (13, "ln_in", act_ln_in), (15, "post", act_post)],
        "dve": [(1, "post", dve_post_a), (5, "pre", arg(dve_conv, 1)), (5, "pre", arg(dve_conv, 2)),
                (6, "pre", arg(dve_conv, 3)), (10, "ln_in", dve_ln_in_a), (10, "pre", dve_bc),
                (13, "pre", dve_dt), (13, "ln_in", dve_ln_in_b), (13, "post", dve_post_b), (15, "post", dve_post_c)],
        "pool": [(2, "late", pool_post_a), (2, "late", pool_post_b), (4, "late", pool_post_c), (14, "pre", pool_dtu)],
    }
    STEPS = {"pe": pe_steps, "act": act_steps, "dve": dve_steps, "pool": pool_steps}
    BEGIN = {"pe": pe_begin, "act": act_begin}
    LAST = {"pe": nsum, "dve": cmul}

    def step_of(c, nxt, n):
        return (c, n) if n < NS else (nxt, n - NS)

    def unit(i, k):
        c = At(i if k < UNITS else i + 1, k)
        c.batch = c.i * QUAD + c.z
        c.unit = c.i * UNITS + c.k
        return c

    def program(e, which):
        def piece(f, c, latest):
            f(e, c, latest) if f is pe_out else f(e, c)

        def pieces(kind_now, c):
            for _, kind, f in PIECES[which]:
                if kind == kind_now:
                    piece(f, c, unit(c.i, UNITS))

        for kind, c in (("ln_in", unit(0, 0)), ("ln_in", unit(0, 1)), ("pre", unit(0, 0))):
            pieces(kind, c)
        if which in BEGIN:
            BEGIN[which](e, unit(0, 0))
        with e.Fori(0, B // QUAD) as i:
            for k in range(UNITS):
                c, nxt, after = unit(i, k), unit(i, k + 1), unit(i, k + 2)
                before = unit(i, k - 1) if k else None
                late = unit(i, k - 2) if k > 1 else None

                def hooks(n):
                    for at, kind, f in PIECES[which]:
                        if at != n:
                            continue
                        if kind == "pre":
                            f(e, nxt)
                        elif kind == "ln_in" and after.l == 0:
                            f(e, after)
                        elif kind == "post" and before is not None:
                            piece(f, before, nxt)
                        elif kind == "late" and late is not None:
                            f(e, late)

                STEPS[which](e, before, c, nxt, hooks)
            if which in LAST:
                LAST[which](e, unit(i, UNITS - 1), NS - 1)
            pieces("late", unit(i, UNITS - 2))
            pieces("post", unit(i, UNITS - 1))
            pieces("late", unit(i, UNITS - 1))

    def dve_setup(e):
        e.memset(a[:].rearrange("p s (h t) -> p (s h) t", h=H)[:, :, 0:1], 0.0).then_inc(setup, 1)
        e.memset(xcp[:, :, 0:KC - 1], 0.0).then_inc(setup, 1)
        e.memset(X[:, B * BLK:], 0.0).then_inc(setup, 1)
        ln_in.setup(e).then_inc(setup, 1)
        ln_out.setup(e).then_inc(setup, 1)
        for s in (scan_done, cmul_done, pre_dve, post_dve, ln_out.dve_done):
            e.sem_inc(s, CREDIT)
        e.wait_ge(loaded, 16 * loads)
        e.tensor_copy(sel[:], w["id2"][:, :].rearrange("p (n o) -> p n o", o=1).to_broadcast([64, 2 * NS, P]))\
            .then_inc(setup, 1)
        e.wait_ge(setup, 7)
        e.tensor_scalar(Aneg[:], Aneg[:], -1.0, None, ALU.mult).then_inc(setup, 1)

    def act_setup(e):
        for s in (bcopy_done, exp_done, pre_act):
            e.sem_inc(s, CREDIT)
        e.wait_ge(loaded, 16 * loads)
        e.preload_act_table_set("natural_log_exp_and_others")
        e.activation(Aneg[:], w["alog"][:], ACT.Exp).then_inc(setup, 1)
        e.wait_ge(setup, 8)

    def pe_setup(e):
        for s in (rep_b_done, rep_c_done, nsum_done, pre_pe, post_pe):
            e.sem_inc(s, CREDIT)
        e.wait_ge(loaded, 16 * loads)
        e.wait_ge(setup, 8)

    def pool_setup(e):
        for s in (drive_done, pre_pool, post_pool):
            e.sem_inc(s, CREDIT)
        e.wait_ge(loaded, 16 * loads)
        e.wait_ge(setup, 8)

    setups = {"pe": pe_setup, "act": act_setup, "dve": dve_setup, "pool": pool_setup}

    def run(e, which):
        setups[which](e)
        if which == "dve":
            e.wait_ge(setup, 8)
        program(e, which)

    return run


E_, F_ = 8, 344
HT = [128, 128, F_ - 256]
WCOL = 2 * F_ + 3 * D
HEADS, DH = 16, 8
GROUPS = 4
NEG = -1e30


def f32(ap):
    return ap.bitcast(F32)


def barrier(e, phase_end, n):
    e.drain().then_inc(phase_end, 1)
    e.wait_ge(phase_end, 4 * n)


def ffn_phase(sb, psum, sem, held, X, ident, wh, wl, ws, bs, iota8, sel8):
    CREDIT = 80
    NM = 3 * E_
    TURN = 4
    ln = LayerNorm("ffn_ln", sb, sem, held)
    xn = sb("ffn_xn", [P, BLK])
    xf = sb("ffn_xT", [P, T])
    xh = sb("ffn_xT_hi", [P, 2, T], F32R)
    xl = sb("ffn_xT_lo", [P, 2, T], F32R)
    lg = sb("logits", [P, S, E_])
    top = sb("top", [P, S, 8])
    idx = sb("top_index", [P, S, 8], U32)
    idf = sb("top_index_f", [P, S, 2])
    wt = sb("top_weight", [P, 5, S, 1])
    cmb = sb("combine", [P, 2, S, E_])
    cc = sb("combine_split", [40, 2, T], F32R)
    sg = sb("silu_gate", [P, 2, T])
    hf = sb("hidden", [P, 3, T])
    hh = sb("hidden_hi", [P, 3, T], F32R)
    hl = sb("hidden_lo", [P, 3, T], F32R)
    cbs = sb("combine_rows", [P, 2, T])
    ot = sb("expert_out", [P, 2, T])
    ya = sb("ffn_acc", [P, 2, T])
    G = [psum(f"gate{j}", [P, T]) for j in range(2)]
    U = [psum(f"up{j}", [P, T]) for j in range(2)]
    O = [psum(f"down{j}", [P, T]) for j in range(2)]
    CB = psum("combine_ps", [P, T])
    M = psum("ffn_pre_ps", [P, T])
    gate_done, up_done, down_done, cb_done, ytr_done = (sem(n) for n in (
        "gate_done", "up_done", "down_done", "cb_done", "ytr_done"))
    silu_done, hi_done, cbcopy_done = sem("silu_done"), sem("hi_done"), sem("cbcopy_done")
    prod_done, oscale_done, xadd_done = sem("prod_done"), sem("oscale_done"), sem("xadd_done")
    lo_done, yadd_done = sem("lo_done"), sem("yadd_done")
    fpre_pe, fpre_act, fpre_dve, ffn_setup = (sem(n) for n in ("fpre_pe", "fpre_act", "fpre_dve", "ffn_setup"))
    PPE, PACT, PDVE = 3, 4, 17

    class Tile:
        def __init__(self, f, i, k):
            self.b = i * TURN + k
            self.q = k % 2
            self.t = self.b + f * B
            self.p = self.b + f * (B + 1)
            self.n = self.b + f * (B + 2)

    def wait(e, s, v):
        e.wait_ge(s, v + CREDIT)

    def xsrc(c):
        return lambda s: X[:, bass.ds(c.b * BLK + s * D, D)]

    def dve_norm_a(e, c):
        ln.stats(e, c.n, xsrc(c))

    def act_norm(e, c):
        e.preload_act_table_set("natural_log_exp_and_others")
        ln.act(e, c.n)

    def dve_norm_b(e, c):
        ln.apply(e, c.n, xsrc(c), lambda s: xn[:, s * D:(s + 1) * D])

    def pe_xtr(e, c, added):
        e.wait_ge(ln.dve_done, c.n * LayerNorm.NDVE + 16)
        wait(e, fpre_act, c.p * PACT)
        wait(e, fpre_dve, c.p * PDVE)
        wait(e, xadd_done, added)
        for s in range(S):
            m = e.transpose(M[:, s * P:(s + 1) * P], xn[:, s * D:(s + 1) * D], ident[:])
        m.then_inc(fpre_pe, 1)

    def act_x(e, c):
        wait(e, fpre_pe, c.p * PPE + 1)
        wait(e, up_done, (c.t - 1) * NM)
        e.activation(xh[:, c.q, :], M[:], ACT.Copy).then_inc(fpre_act, 1)
        e.activation(xf[:], M[:], ACT.Copy).then_inc(fpre_act, 1)

    def dve_x(e, c):
        wait(e, fpre_act, c.p * PACT + 2)
        e.tensor_tensor(xl[:, c.q, :], M[:], f32(xh[:, c.q, :]), ALU.subtract).then_inc(fpre_dve, 1)

    def pe_logits(e, c):
        wait(e, fpre_dve, c.p * PDVE + 1)
        for s in range(S):
            m = e.matmul(M[:, s * E_:(s + 1) * E_], xf[:, s * P:(s + 1) * P], ws[:], start=True, stop=True)
        m.then_inc(fpre_pe, 1)

    def dve_route_a(e, c):
        base = c.p * PDVE
        wait(e, fpre_pe, c.p * PPE + 2)
        e.tensor_tensor(lg[:], M[:, 0:S * E_].rearrange("p (s n) -> p s n", s=S),
                        bs[:].rearrange("p (o n) -> p o n", o=1).to_broadcast([P, S, E_]), ALU.add)\
            .then_inc(fpre_dve, 1)
        hold(e, fpre_dve, base + 2 + CREDIT, held)
        for s in range(S):
            e.max(out=top[:, s, :], in_=lg[:, s, :]).then_inc(fpre_dve, 1)
        for s in range(S):
            hold(e, fpre_dve, base + 3 + s + CREDIT, held)
            e.max_index(out=idx[:, s, :], in_max=top[:, s, :], in_values=lg[:, s, :]).then_inc(fpre_dve, 1)
        wait(e, fpre_dve, base + 10)
        e.tensor_copy(idf[:], idx[:, :, 0:2]).then_inc(fpre_dve, 1)
        e.tensor_tensor(wt[:, 0], top[:, :, 1:2], top[:, :, 0:1], ALU.subtract).then_inc(fpre_dve, 1)

    def act_route(e, c):
        wait(e, fpre_dve, c.p * PDVE + 12)
        e.activation(wt[:, 1], wt[:, 0], ACT.Exp).then_inc(fpre_act, 1)

    def dve_route_b(e, c):
        base = c.p * PDVE
        it = iota8[:].rearrange("p (o n) -> p o n", o=1).to_broadcast([P, S, E_])
        wait(e, fpre_act, c.p * PACT + 3)
        e.tensor_scalar(wt[:, 2], wt[:, 1], 1.0, None, ALU.add).then_inc(fpre_dve, 1)
        wait(e, fpre_dve, base + 13)
        e.reciprocal(wt[:, 3], wt[:, 2]).then_inc(fpre_dve, 1)
        wait(e, fpre_dve, base + 14)
        e.tensor_tensor(wt[:, 4], wt[:, 3], wt[:, 1], ALU.mult).then_inc(fpre_dve, 1)
        wait(e, fpre_pe, (c.p - 1) * PPE + 3)
        e.tensor_tensor(cmb[:, 0], it, idf[:, :, 0:1].to_broadcast([P, S, E_]), ALU.is_equal).then_inc(xr, 1)
        e.tensor_tensor(cmb[:, 1], it, idf[:, :, 1:2].to_broadcast([P, S, E_]), ALU.is_equal).then_inc(xr, 1)
        wait(e, fpre_dve, base + 15)
        e.wait_ge(xr, c.p * 4 + 2)
        e.tensor_tensor(cmb[:, 0], cmb[:, 0], wt[:, 3].to_broadcast([P, S, E_]), ALU.mult).then_inc(xr, 1)
        e.tensor_tensor(cmb[:, 1], cmb[:, 1], wt[:, 4].to_broadcast([P, S, E_]), ALU.mult).then_inc(xr, 1)
        e.wait_ge(xr, c.p * 4 + 4)
        e.tensor_tensor(cmb[:, 0], cmb[:, 0], cmb[:, 1], ALU.add).then_inc(fpre_dve, 1)

    xr = sem("route_steps")

    def pe_ctr(e, c):
        wait(e, fpre_dve, c.p * PDVE + 16)
        for s in range(S):
            m = e.transpose(M[0:E_, s * P:(s + 1) * P], cmb[:, 0, s, :], ident[:])
        m.then_inc(fpre_pe, 1)

    def act_c(e, c):
        wait(e, fpre_pe, c.p * PPE + 3)
        wait(e, cb_done, (c.t - 1) * E_)
        e.activation(cc[0:E_, c.q, :], M[0:E_, :], ACT.Copy).then_inc(fpre_act, 1)

    def dve_c(e, c):
        wait(e, fpre_act, c.p * PACT + 4)
        e.tensor_tensor(cc[32:40, c.q, :], M[0:E_, :], f32(cc[0:E_, c.q, :]), ALU.subtract).then_inc(fpre_dve, 1)

    def part(m):
        return HT[m % 3]

    def three(e, out, w_sl, q, kind):
        e.matmul(out, wh(kind, w_sl), xh[:, q, :], start=True, stop=False)
        e.matmul(out, wl(kind, w_sl), xh[:, q, :], start=False, stop=False)
        return e.matmul(out, wh(kind, w_sl), xl[:, q, :], start=False, stop=True)

    def step_of(before, c, m):
        if m >= 0:
            return c, m
        return (before, m + NM) if before is not None else None

    def pe_down(e, c, m):
        j, ex = m % 3, m // 3
        rows = part(m)
        wait(e, hi_done, c.t * NM + m + 1)
        if j == 0:
            wait(e, oscale_done, c.t * E_ + ex - 1)
        out = O[ex % 2][:]
        e.matmul(out, wh("down", (ex, j, rows)), hh[0:rows, m % 3, :], start=(j == 0), stop=False)
        e.matmul(out, wl("down", (ex, j, rows)), hh[0:rows, m % 3, :], start=False, stop=False)
        wait(e, lo_done, c.t * NM + m + 1)
        e.matmul(out, wh("down", (ex, j, rows)), hl[0:rows, m % 3, :], start=False, stop=(j == 2))\
            .then_inc(down_done, 1)

    def pe_ytr(e, c, read):
        wait(e, yadd_done, c.t * E_ + E_)
        wait(e, fpre_dve, read * PDVE)
        for s in range(S):
            m = e.transpose(M[:, s * P:(s + 1) * P], ya[:, c.q, s * P:(s + 1) * P], ident[:])
        m.then_inc(ytr_done, 1)

    def pe_tile(e, before, c, hooks):
        wait(e, fpre_dve, c.p * PDVE + 17)
        for m in range(NM):
            j, ex, rows = m % 3, m // 3, part(m)
            if j == 0:
                wait(e, cbcopy_done, c.t * E_ + ex)
                e.matmul(CB[:], sel8[:, ex, :], cc[:, c.q, :], start=True, stop=True).then_inc(cb_done, 1)
            wait(e, silu_done, c.t * NM + m - 1)
            three(e, G[m % 2][0:rows, :], (ex, j, rows), c.q, "gate").then_inc(gate_done, 1)
            wait(e, prod_done, c.t * NM + m - 1)
            three(e, U[m % 2][0:rows, :], (ex, j, rows), c.q, "up").then_inc(up_done, 1)
            if step_of(before, c, m - 2):
                pe_down(e, *step_of(before, c, m - 2))
            if m == YTR and before is not None:
                pe_ytr(e, before, c.p + 1)
            hooks(m)

    def pe_end(e, c):
        pe_down(e, c, NM - 2)
        pe_down(e, c, NM - 1)
        pe_ytr(e, c, c.p + 2)

    def act_hi(e, c, m):
        rows = part(m)
        wait(e, prod_done, c.t * NM + m + 1)
        wait(e, down_done, c.t * NM + m - 2)
        e.activation(hh[0:rows, m % 3, :], hf[0:rows, m % 3, :], ACT.Copy).then_inc(hi_done, 1)

    def act_tile(e, before, c, hooks):
        for m in range(NM):
            rows = part(m)
            if step_of(before, c, m - 1):
                act_hi(e, *step_of(before, c, m - 1))
            wait(e, gate_done, c.t * NM + m + 1)
            wait(e, prod_done, c.t * NM + m - 1)
            e.activation(sg[0:rows, m % 2, :], G[m % 2][0:rows, :], ACT.Silu).then_inc(silu_done, 1)
            if m % 3 == 1:
                ex = m // 3
                wait(e, cb_done, c.t * E_ + ex + 1)
                wait(e, oscale_done, c.t * E_ + ex - 1)
                e.activation(cbs[:, ex % 2, :], CB[:], ACT.Copy).then_inc(cbcopy_done, 1)
            hooks(m)

    def act_end(e, c):
        act_hi(e, c, NM - 1)

    def dve_oscale(e, c, ex):
        wait(e, down_done, c.t * NM + 3 * ex + 3)
        wait(e, cbcopy_done, c.t * E_ + ex + 1)
        wait(e, yadd_done, c.t * E_ + ex - 1)
        e.tensor_tensor(ot[:, ex % 2, :], O[ex % 2][:], cbs[:, ex % 2, :], ALU.mult).then_inc(oscale_done, 1)

    def dve_xadd(e, c):
        wait(e, ytr_done, c.t + 1)
        xb = X[:, bass.ds(c.b * BLK, BLK)]
        e.tensor_tensor(xb, xb, M[:], ALU.add).then_inc(xadd_done, 1)

    def dve_tile(e, before, c, hooks):
        for m in range(NM):
            rows = part(m)
            wait(e, silu_done, c.t * NM + m + 1)
            wait(e, up_done, c.t * NM + m + 1)
            wait(e, lo_done, c.t * NM + m - 2)
            e.tensor_tensor(hf[0:rows, m % 3, :], U[m % 2][0:rows, :], sg[0:rows, m % 2, :], ALU.mult)\
                .then_inc(prod_done, 1)
            if m % 3 == 2 and step_of(before, c, m - 5):
                cc, mm = step_of(before, c, m - 5)
                dve_oscale(e, cc, mm // 3)
            if m == YTR + 1 and before is not None:
                dve_xadd(e, before)
            hooks(m)

    def dve_end(e, c):
        dve_oscale(e, c, E_ - 1)
        dve_xadd(e, c)

    def pool_yadd(e, c, ex):
        hold(e, oscale_done, c.t * E_ + ex + 1 + CREDIT, held)
        y = ya[:, c.q, :]
        if ex == 0:
            e.tensor_copy(y, ot[:, 0, :]).then_inc(yadd_done, 1)
        else:
            wait(e, yadd_done, c.t * E_ + ex)
            e.tensor_tensor(y, y, ot[:, ex % 2, :], ALU.add).then_inc(yadd_done, 1)

    def pool_tile(e, before, c, hooks):
        for m in range(NM):
            rows = part(m)
            wait(e, hi_done, c.t * NM + m + 1)
            wait(e, down_done, c.t * NM + m - 2)
            e.tensor_tensor(hl[0:rows, m % 3, :], hf[0:rows, m % 3, :], f32(hh[0:rows, m % 3, :]), ALU.subtract)\
                .then_inc(lo_done, 1)
            if m % 3 == 0 and step_of(before, c, m - 6):
                cc, mm = step_of(before, c, m - 6)
                pool_yadd(e, cc, mm // 3)
            hooks(m)

    def pool_end(e, c):
        pool_yadd(e, c, E_ - 2)
        pool_yadd(e, c, E_ - 1)

    YTR = 5
    AHEAD = (dve_norm_a, act_norm)
    PIECES = {
        "pe": [(10, pe_xtr), (12, pe_logits), (18, pe_ctr)],
        "act": [(11, act_x), (15, act_norm), (15, act_route), (19, act_c)],
        "dve": [(8, dve_norm_b), (11, dve_x), (12, dve_norm_a), (14, dve_route_a), (16, dve_route_b), (21, dve_c)],
        "pool": [],
    }
    TILES = {"pe": pe_tile, "act": act_tile, "dve": dve_tile, "pool": pool_tile}
    END = {"pe": pe_end, "act": act_end, "dve": dve_end, "pool": pool_end}
    OWN = {"pe": (gate_done, up_done, down_done, cb_done, ytr_done, fpre_pe),
           "act": (silu_done, hi_done, cbcopy_done, fpre_act),
           "dve": (prod_done, oscale_done, xadd_done, fpre_dve), "pool": (lo_done, yadd_done)}

    def credits(e, which):
        for s in OWN[which]:
            e.sem_inc(s, CREDIT)

    def run(e, which, f, weights=None):
        if which == "dve":
            ln.setup(e).then_inc(ffn_setup, 1)
            e.memset(f32(cc[:]), 0.0).then_inc(ffn_setup, 1)
        e.wait_ge(ffn_setup, 2 * (f + 1))
        def piece(p, c, after, added):
            if p is pe_xtr:
                p(e, c, added)
            else:
                p(e, after if p in AHEAD else c)

        first, second = Tile(f, 0, 0), Tile(f, 0, 1)
        if which == "dve":
            dve_norm_a(e, first)
        if which == "act":
            act_norm(e, first)
            if weights:
                weights(e, which, -1)
        for n, (_, p) in enumerate(PIECES[which]):
            piece(p, first, second, first.t)
            if weights:
                weights(e, which, n)
        with e.Fori(0, B // TURN) as i:
            for k in range(TURN):
                nxt, after = Tile(f, i, k + 1), Tile(f, i, k + 2)
                before = Tile(f, i, k - 1) if k else None

                def hooks(m):
                    for at, p in PIECES[which]:
                        if at == m:
                            piece(p, nxt, after, nxt.t - 1)

                TILES[which](e, before, Tile(f, i, k), hooks)
            END[which](e, Tile(f, i, TURN - 1))
        if which == "dve":
            dve_norm_b(e, Tile(f, 0, B + 1))

    return run, credits


def attention_phase(sb, psum, sem, held, X, ident, w):
    CREDIT = 80
    NT = HEADS * S
    NQ = GROUPS * S
    PER = NT // GROUPS
    TURN = 4
    ln = LayerNorm("att_ln", sb, sem, held)
    xn = sb("att_xn", [P, BLK])
    xh = sb("att_xT_hi", [P, T], F32R)
    xl = sb("att_xT_lo", [P, T], F32R)
    qf = sb("qk_full", [P, T])
    qh = sb("qk_hi", [P, T], F32R)
    qk = sb("qk_parts", [P, 2, GROUPS, T], F32R)
    V = sb("v_padded", [P, S, GROUPS, 4, 32])
    bias = sb("alibi", [P, HEADS, T])
    pn = w["probs"]
    nm = sb("neg_max", [P, NT])
    rs = sb("row_sum", [P, NT])
    ri = sb("row_sum_inv", [P, NT])
    PT = sb("probs_T", [P, 2, 4, T])
    rx = sb("row_sum_inv_wide", [P, S, 4, 32])
    rr = sb("row_sum_inv_T", [P, T])
    yn = sb("att_out_T", [P, GROUPS, T])
    SB = [psum(f"score{j}", [P, T]) for j in range(3)]
    TB = [psum(f"probs_t{j}", [P, T]) for j in range(2)]
    Y = [psum(f"att_y{j}", [P, T]) for j in range(2)]
    M = psum("att_pre_ps", [P, T])
    xtr_done, vp_done, proj_done, score_done, tr_done, pv_done, rtr_done, out_done = (sem(n) for n in (
        "att_xtr", "v_proj_done", "qk_done", "score_done", "tr_done", "pv_done", "rtr_done", "out_done"))
    x_hi, qf_done, exp_done, evac_act, rr_done = (sem(n) for n in (
        "att_x_hi", "qf_done", "att_exp", "evac_act", "rr_done"))
    x_lo, parts_done, v_done, max_done, evac_dve, ri_done, rx_done, yn_done, xadd = (sem(n) for n in (
        "att_x_lo", "parts_done", "v_done", "max_done", "evac_dve", "ri_done", "rx_done", "yn_done", "att_xadd"))
    qh_done, bp_added = sem("qh_done"), sem("proj_bias_added")
    setup = sem("att_setup")
    OFF = [384 - P * b for b in range(S)]

    LAG = {"pe_transposes": 1, "act_evac": 1, "dve_evac": 2}
    SLOT = {"pe_pv": 3, "pe_v": 1, "dve_v": 6,
            "pe_proj6": 7, "act_proj6": 7, "dve_proj6": 11, "pe_proj7": 16, "act_proj7": 16, "dve_proj7": 21,
            "dve_stats": 9, "act_ln": 12, "dve_norm": 14, "pe_x": 21, "act_x": 22, "dve_x": 22,
            "dve_inverse": 3, "pe_norm": 6, "act_rows": 7, "dve_normed": 9, "pe_out": 10, "dve_xadd": 15,
            "pe_q": 9, "act_q": 10, "dve_q": 13, "pe_k": 13, "act_k": 13, "dve_k": 15}

    def wait(e, s, v):
        e.wait_ge(s, v + CREDIT)

    def lagged(before, b, t):
        if t >= 0:
            return b, t
        return (before, t + NT) if before is not None else None

    def group_of(t, name):
        n = t - SLOT[name]
        return n // PER - 1 if n % PER == 0 and n >= PER else None

    def projections(b, n):
        return b * (2 * GROUPS) + n

    def pe_x(e, b):
        e.wait_ge(ln.dve_done, b * LayerNorm.NDVE + 16)
        wait(e, qf_done, projections(b, 0))
        for s in range(S):
            m = e.transpose(M[:, s * P:(s + 1) * P], xn[:, s * D:(s + 1) * D], ident[:])
        m.then_inc(xtr_done, 1)

    def pe_proj(e, b, n):
        if n == 0:
            wait(e, x_lo, b + 1)
        wait(e, qf_done, projections(b, n))
        wgt = w["qkh"][:, n % 2, n // 2, :], w["qkl"][:, n % 2, n // 2, :]
        e.matmul(M[:], wgt[0], xh[:], start=True, stop=False)
        e.matmul(M[:], wgt[1], xh[:], start=False, stop=False)
        e.matmul(M[:], wgt[0], xl[:], start=False, stop=True).then_inc(proj_done, 1)

    def pe_v(e, b):
        wait(e, qf_done, projections(b, 6))
        wait(e, xadd, b - 1)
        for s in range(S):
            sub = slice(s * P, (s + 1) * P)
            e.matmul(M[:, sub], xh[:, sub], w["vh"][:], start=True, stop=False)
            e.matmul(M[:, sub], xl[:, sub], w["vh"][:], start=False, stop=False)
            m = e.matmul(M[:, sub], xh[:, sub], w["vl"][:], start=False, stop=True)
        m.then_inc(vp_done, 1)

    def bank(t):
        if t < NT - 1:
            return t % 3, {0: 4, 1: 2}.get(t, 3) if t < 3 else 3
        return (t - 2) % 3, 2

    def pe_score(e, b, t):
        g, qb, G = t % 4, t // 4 % S, t // PER
        place, ago = bank(t)
        if t % PER == 0:
            wait(e, parts_done, projections(b, 2 * G + 2))
        wait(e, max_done, b * NT + t + 1 - ago)
        rows = slice(32 * g, 32 * g + 32)
        e.matmul(SB[place][:, 0:P * (qb + 1)], qk[rows, 0, G, qb * P:(qb + 1) * P],
                 qk[rows, 1, G, 0:P * (qb + 1)], start=True, stop=True).then_inc(score_done, 1)

    def pe_transposes(e, b, t):
        qb = t // 4 % S
        wait(e, exp_done, b * NT + t + 1)
        wait(e, evac_act if t % 2 == 0 else evac_dve, b * (NT // 2) + t // 2)
        for kb in range(qb + 1):
            m = e.transpose(TB[t % 2][:, kb * P:(kb + 1) * P], pn[:, t % 4, kb * P:(kb + 1) * P], ident[:])
        m.then_inc(tr_done, 1)

    def pe_pv(e, b, n):
        G, qb = n // S, n % S
        wait(e, evac_act, b * (NT // 2) + 2 * n + 2)
        wait(e, evac_dve, b * (NT // 2) + 2 * n + 2)
        if n == 0:
            wait(e, v_done, b + 1)
        if qb == 0:
            wait(e, yn_done, b * GROUPS + G - 1)
        for kb in range(qb + 1):
            for g in range(4):
                m = e.matmul(Y[G % 2][32 * g:32 * g + 32, qb * P:(qb + 1) * P], V[:, kb, G, g, :],
                             PT[:, n % 2, g, kb * P:(kb + 1) * P], start=(kb == 0), stop=(kb == qb))
        m.then_inc(pv_done, 1)

    def pe_norm(e, b, G, ahead):
        wait(e, rx_done, b * GROUPS + G + 1)
        if G == GROUPS - 1 and ahead:
            wait(e, v_done, b + 2)
        elif G == 0:
            wait(e, x_lo, b + 2)
        else:
            wait(e, qf_done, projections(b + 1, 2 * G))
        for qb in range(S):
            m = e.transpose(M[:, qb * P:(qb + 1) * P], rx[:, qb].rearrange("p g d -> p (g d)"), ident[:])
        m.then_inc(rtr_done, 1)

    def pe_out(e, b, s, ahead):
        if s == 0:
            wait(e, yn_done, b * GROUPS + GROUPS)
            wait(e, rr_done, b * GROUPS + GROUPS)
            if ahead:
                wait(e, qf_done, projections(b + 1, 7))
        for G in range(GROUPS):
            m = e.matmul(M[:, s * D:(s + 1) * D], yn[:, G, s * P:(s + 1) * P], w["wp"][:, G, :],
                         start=(G == 0), stop=(G == GROUPS - 1))
        m.then_inc(out_done, 1)

    def pe_begin_x(e):
        pe_x(e, 0)

    def pe_begin(e):
        for n in range(6):
            pe_proj(e, 0, n)
        pe_score(e, 0, 0)
        pe_score(e, 0, 1)

    def pe_batch(e, before, b):
        for t in range(NT):
            pe_score(e, *((b, t + 2) if t + 2 < NT else (b + 1, t + 2 - NT)))
            late = lagged(before, b, t - LAG["pe_transposes"])
            if late:
                pe_transposes(e, *late)
            quad = lagged(before, b, t - SLOT["pe_pv"] - 1)
            if quad and quad[1] % 4 == 3:
                pe_pv(e, quad[0], quad[1] // 4)
            if before is not None:
                if t == SLOT["pe_norm"]:
                    pe_norm(e, before, GROUPS - 1, True)
                if SLOT["pe_out"] <= t < SLOT["pe_out"] + S:
                    pe_out(e, before, t - SLOT["pe_out"], True)
            if t == SLOT["pe_v"]:
                pe_v(e, b)
            if t == SLOT["pe_proj6"]:
                wait(e, v_done, b + 1)
                wait(e, rr_done, b * GROUPS)
                pe_proj(e, b, 6)
            if t == SLOT["pe_proj7"]:
                wait(e, xadd, b)
                pe_proj(e, b, 7)
            if t == SLOT["pe_x"]:
                pe_x(e, b + 1)
            if group_of(t, "pe_norm") is not None:
                pe_norm(e, b, group_of(t, "pe_norm"), False)
            for k, name in enumerate(("pe_q", "pe_k")):
                G = group_of(t, name)
                if G is not None:
                    wait(e, rr_done, b * GROUPS + G + 1)
                    pe_proj(e, b + 1, 2 * G + k)

    def pe_end(e, b):
        for t in range(NT - LAG["pe_transposes"], NT):
            pe_transposes(e, b, t)
        for t in range(NT - SLOT["pe_pv"] - 1, NT):
            if t % 4 == 3:
                pe_pv(e, b, t // 4)
        pe_norm(e, b, GROUPS - 1, False)
        for s in range(S):
            pe_out(e, b, s, False)

    def act_x(e, b):
        wait(e, xtr_done, b + 1)
        e.activation(xh[:], M[:], ACT.Copy).then_inc(x_hi, 1)

    def act_proj(e, b, n):
        wait(e, proj_done, projections(b, n + 1))
        wait(e, parts_done, projections(b, n))
        bq, scale = (w["bqs"], DH ** -0.5) if n % 2 == 0 else (w["bk"], 1.0)
        e.activation(qf[:], M[:], ACT.Identity, bias=bq[:, n // 2:n // 2 + 1], scale=scale).then_inc(qf_done, 1)

    def act_exp(e, b, t):
        wait(e, max_done, b * NT + t + 1)
        p = pn[:, t % 4, 0:P * (t // 4 % S + 1)]
        e.activation(p, p, ACT.Exp, bias=nm[:, t:t + 1], scale=-1.0, accum_out=rs[:, t:t + 1]).then_inc(exp_done, 1)

    def act_evac(e, b, t):
        qb, n = t // 4 % S, t // 4
        wait(e, tr_done, b * NT + t + 1)
        wait(e, pv_done, b * NQ + n - 1)
        e.activation(PT[:, n % 2, t % 4, 0:P * (qb + 1)], TB[t % 2][:, 0:P * (qb + 1)], ACT.Copy)\
            .then_inc(evac_act, 1)

    def act_rows(e, b, G):
        wait(e, rtr_done, b * GROUPS + G + 1)
        wait(e, yn_done, b * GROUPS + G)
        e.activation(rr[:], M[:], ACT.Copy).then_inc(rr_done, 1)

    def act_begin_x(e):
        e.preload_act_table_set("natural_log_exp_and_others")
        ln.act(e, 0)
        act_x(e, 0)

    def act_begin(e):
        for n in range(6):
            act_proj(e, 0, n)

    def act_batch(e, before, b):
        for t in range(NT):
            act_exp(e, b, t)
            late = lagged(before, b, t - LAG["act_evac"])
            if late and late[1] % 2 == 0:
                act_evac(e, *late)
            if t == SLOT["act_rows"] and before is not None:
                act_rows(e, before, GROUPS - 1)
            if t == SLOT["act_proj6"]:
                act_proj(e, b, 6)
            if t == SLOT["act_ln"]:
                ln.act(e, b + 1)
            if t == SLOT["act_proj7"]:
                act_proj(e, b, 7)
            if t == SLOT["act_x"]:
                act_x(e, b + 1)
            if group_of(t, "act_rows") is not None:
                act_rows(e, b, group_of(t, "act_rows"))
            for k, name in enumerate(("act_q", "act_k")):
                if group_of(t, name) is not None:
                    act_proj(e, b + 1, 2 * group_of(t, name) + k)

    def act_end(e, b):
        for t in range(NT - LAG["act_evac"], NT):
            if t % 2 == 0:
                act_evac(e, b, t)
        act_rows(e, b, GROUPS - 1)

    def source(b):
        return lambda s: X[:, bass.ds(b * BLK + s * D, D)]

    def dve_stats(e, b):
        ln.stats(e, b, source(b))

    def dve_norm(e, b):
        wait(e, xtr_done, b)
        ln.apply(e, b, source(b), lambda s: xn[:, s * D:(s + 1) * D])

    def dve_x(e, b):
        wait(e, x_hi, b + 1)
        e.tensor_tensor(xl[:], M[:], f32(xh[:]), ALU.subtract).then_inc(x_lo, 1)

    def dve_proj(e, b, n):
        wait(e, qh_done, projections(b, n + 1))
        wait(e, score_done, b * NT - NT + (n // 2 + 1) * PER)
        e.scalar_tensor_tensor(qk[:, n % 2, n // 2, :], f32(qh[:]), w["minus_lo"][:, n % 2:n % 2 + 1],
                               qf[:], ALU.mult, ALU.add).then_inc(parts_done, 1)

    def dve_v(e, b):
        wait(e, vp_done, b + 1)
        wait(e, pv_done, b * NQ)
        e.tensor_tensor(V[:, :, :, :, 0:DH].rearrange("p s a g d -> p s (a g) d"),
                        M[:].rearrange("p (s n d) -> p s n d", s=S, d=DH),
                        w["bv"][:].rearrange("p (o n d) -> p o n d", o=1, d=DH).to_broadcast([P, S, HEADS, DH]),
                        ALU.add).then_inc(v_done, 1)

    def dve_maxima(e, b, t):
        qb, hd = t // 4 % S, 4 * (t // PER) + t % 4
        wait(e, score_done, b * NT + t + 1)
        hold(e, tr_done, b * NT + t - 3 + CREDIT, held)
        width = P * (qb + 1)
        e.tensor_tensor_reduce(pn[:, t % 4, 0:width], SB[bank(t)[0]][:, 0:width], bias[:, hd, OFF[qb]:T],
                               -1.0, 3.0e38, ALU.add, ALU.min, nm[:, t:t + 1]).then_inc(max_done, 1)

    def dve_evac(e, b, t):
        qb, n = t // 4 % S, t // 4
        wait(e, tr_done, b * NT + t + 1)
        wait(e, pv_done, b * NQ + n - 1)
        e.tensor_copy(PT[:, n % 2, t % 4, 0:P * (qb + 1)], TB[t % 2][:, 0:P * (qb + 1)]).then_inc(evac_dve, 1)

    def dve_inverse(e, b, G):
        wait(e, exp_done, b * NT + PER * G + PER)
        e.reciprocal(ri[:, PER * G:PER * (G + 1)], rs[:, PER * G:PER * (G + 1)]).then_inc(ri_done, 1)
        wait(e, ri_done, b * GROUPS + G + 1)
        wait(e, rtr_done, b * GROUPS + G)
        e.tensor_copy(rx[:], ri[:, PER * G:PER * (G + 1)].rearrange("p (q g o) -> p q g o", q=S, o=1)
                      .to_broadcast([P, S, 4, 32])).then_inc(rx_done, 1)

    def dve_normed(e, b, G):
        wait(e, rr_done, b * GROUPS + G + 1)
        wait(e, pv_done, b * NQ + S * G + S)
        e.tensor_tensor(yn[:, G, :], Y[G % 2][:], rr[:], ALU.mult).then_inc(yn_done, 1)

    def dve_xadd(e, b):
        wait(e, out_done, (b + 1) * S)
        wait(e, bp_added, b + 1)
        xb = X[:, bass.ds(b * BLK, BLK)]
        e.tensor_tensor(xb, xb, M[:], ALU.add).then_inc(xadd, 1)

    def dve_begin_x(e):
        dve_stats(e, 0)
        dve_norm(e, 0)
        dve_x(e, 0)

    def dve_begin(e):
        for n in range(6):
            dve_bias(e, 3 * n)
            dve_proj(e, 0, n)
        e.wait_ge(setup, 3 + HEADS)

    def dve_batch(e, before, b):
        for t in range(NT):
            dve_maxima(e, b, t)
            late = lagged(before, b, t - LAG["dve_evac"])
            if late and late[1] % 2 == 1:
                dve_evac(e, *late)
            if before is not None:
                if t == SLOT["dve_inverse"]:
                    dve_inverse(e, before, GROUPS - 1)
                if t == SLOT["dve_normed"]:
                    dve_normed(e, before, GROUPS - 1)
                if t == SLOT["dve_xadd"]:
                    dve_xadd(e, before)
            if t == SLOT["dve_v"]:
                dve_v(e, b)
            if t == SLOT["dve_proj6"]:
                dve_proj(e, b, 6)
            if t == SLOT["dve_stats"]:
                dve_stats(e, b + 1)
            if t == SLOT["dve_norm"]:
                dve_norm(e, b + 1)
            if t == SLOT["dve_proj7"]:
                dve_proj(e, b, 7)
            if t == SLOT["dve_x"]:
                dve_x(e, b + 1)
            if group_of(t, "dve_inverse") is not None:
                dve_inverse(e, b, group_of(t, "dve_inverse"))
            if group_of(t, "dve_normed") is not None:
                dve_normed(e, b, group_of(t, "dve_normed"))
            for k, name in enumerate(("dve_q", "dve_k")):
                if group_of(t, name) is not None:
                    dve_proj(e, b + 1, 2 * group_of(t, name) + k)

    def dve_end(e, b):
        for t in range(NT - LAG["dve_evac"], NT):
            if t % 2 == 1:
                dve_evac(e, b, t)
        dve_inverse(e, b, GROUPS - 1)
        dve_normed(e, b, GROUPS - 1)
        dve_xadd(e, b)

    def pool_round(e, b, n):
        hold(e, qf_done, projections(b, n + 1) + CREDIT, held)
        hold(e, parts_done, projections(b, n) + CREDIT, held)
        e.tensor_copy(qh[:], qf[:]).then_inc(qh_done, 1)

    def pool_begin(e):
        for n in range(6):
            pool_round(e, 0, n)

    def pool_batch(e, before, b):
        pool_round(e, b, 6)
        pool_round(e, b, 7)
        e.wait_ge(ln.dve_done, (b + 1) * LayerNorm.NDVE)
        xb = X[:, bass.ds(b * BLK, BLK)].rearrange("p (s d) -> p s d", s=S)
        e.tensor_tensor(xb, xb, w["bp"][:].rearrange("p (o d) -> p o d", o=1).to_broadcast([P, S, D]), ALU.add)\
            .then_inc(bp_added, 1)
        for n in range(6):
            pool_round(e, b + 1, n)

    OWN = {"pe": (xtr_done, vp_done, proj_done, score_done, tr_done, pv_done, rtr_done, out_done),
           "act": (x_hi, qf_done, exp_done, evac_act, rr_done),
           "dve": (x_lo, parts_done, v_done, max_done, evac_dve, ri_done, rx_done, yn_done, xadd),
           "pool": (qh_done, bp_added)}
    BEGIN_X = {"pe": pe_begin_x, "act": act_begin_x, "dve": dve_begin_x}
    BEGIN = {"pe": pe_begin, "act": act_begin, "dve": dve_begin, "pool": pool_begin}
    BATCH = {"pe": pe_batch, "act": act_batch, "dve": dve_batch, "pool": pool_batch}
    END = {"pe": pe_end, "act": act_end, "dve": dve_end}

    def dve_bias(e, first):
        for hd in range(first, min(first + 3, HEADS)):
            e.scalar_tensor_tensor(bias[:, hd, :], w["rel"], w["slopes"][:, hd:hd + 1], w["mask"],
                                   ALU.mult, ALU.add).then_inc(setup, 1)

    def run(e, which, weights):
        for s in OWN[which]:
            e.sem_inc(s, CREDIT)
        if which == "dve":
            ln.setup(e).then_inc(setup, 1)
            e.memset(V[:], 0.0).then_inc(setup, 1)
        e.wait_ge(setup, 2)
        if which in BEGIN_X:
            BEGIN_X[which](e)
        weights(e, which)
        if which == "dve":
            e.tensor_scalar(w["bqs"][:], w["bq"][:], DH ** -0.5, None, ALU.mult).then_inc(setup, 1)
        e.wait_ge(setup, 3)
        if which in BEGIN:
            BEGIN[which](e)
        with e.Fori(0, B // TURN) as i:
            for k in range(TURN):
                BATCH[which](e, i * TURN + k - 1 if k else None, i * TURN + k)
            if which in END:
                END[which](e, i * TURN + TURN - 1)

    return run


def build(nc, x, win, cw, cb, xp, dtw, dtb, alog, dskip, wout, lnw, lnb, wqk, bqk, wv, bv, wp, bp, slopes,
          ws, bs, wffn, id_dram, rel, mask, minus_lo, iota, out):
    with ExitStack() as ctx:
        def allocators(c):
            return (lambda name, shape, dt=F32: c.enter_context(nc.sbuf_tensor(name, shape, dt)),
                    lambda name, shape, dt=F32: c.enter_context(nc.psum_tensor(name, shape, dt)))

        def sem(name):
            return ctx.enter_context(nc.semaphore(name))

        def row(a):
            n = a.shape[0]
            return a.rearrange("(o n) -> o n", o=1).to_broadcast([P, n])

        sb, psum = allocators(ctx)
        X = sb("stream", [P, (B + 2) * BLK])
        ident = sb("ident", [P, P])
        loaded, stored, phase_end, held = sem("loaded"), sem("stored"), sem("phase_end"), sem("held")
        sel8 = sb("expert_select", [40, E_, P], F32R)
        small = {"ws": sb("w_router", [P, E_]), "bs": sb("b_router", [P, E_]), "iota": sb("iota", [P, E_])}
        with ExitStack() as c1:
            sb1, psum1 = allocators(c1)
            w = {"in": sb1("w_in", [P, L, 2 * DI]), "cw": sb1("w_conv", [P, L, H, KC]), "cb": sb1("b_conv", [P, L, H]),
                 "xp": sb1("w_xp", [P, L, H, 40]), "dt": sb1("w_dt", [64, L, DI]), "dtb": sb1("b_dt", [P, L, H]),
                 "alog": sb1("a_log", [P, L, H, NS]), "D": sb1("d_skip", [P, L, H]), "out": sb1("w_out", [P, L, H, D]),
                 "lnw": sb1("ln_w", [P, L, D]), "lnb": sb1("ln_b", [P, L, D]), "id2": sb1("id2", [64, 32])}
            flat = lambda t: t[:].rearrange("p l d -> p (l d)")
            loads = [(X[:, 0:B * BLK].rearrange("p (n d) -> p n d", d=D), x.rearrange("b (s p) d -> p (b s) d", p=P)),
                     (ident[:], id_dram), (w["in"][:], win), (w["cw"][:], cw), (w["cb"][:], cb), (w["xp"][:], xp),
                     (w["dt"][32:40], dtw), (w["dtb"][:], dtb), (w["alog"][:], alog), (w["D"][:], dskip),
                     (w["out"][:], wout), (flat(w["lnw"]), row(lnw.rearrange("l d -> (l d)"))),
                     (flat(w["lnb"]), row(lnb.rearrange("l d -> (l d)"))),
                     (w["id2"][0:32], id_dram[0:32, 0:32]), (w["id2"][32:64], id_dram[0:32, 0:32]),
                     (small["ws"][:], ws), (small["bs"][:], row(bs)), (small["iota"][:], iota)]
            mamba = mamba_phase(sb1, psum1, sem, held, X, w, ident, loaded, len(loads))

        WH, WL = sb("ffn_w_hi", [P, E_, WCOL], F32R), sb("ffn_w_lo", [P, E_, WCOL], F32R)

        def ffn_w(t):
            def get(kind, at):
                ex, j, rows = at
                if kind == "down":
                    return t[0:rows, ex, 2 * F_ + j * D:2 * F_ + (j + 1) * D]
                first = (F_ if kind == "up" else 0) + j * P
                return t[:, ex, first:first + rows]
            return get

        with ExitStack() as c2:
            sb2, _ = allocators(c2)
            raw = sb2("raw_weights", [P, E_, WCOL])
            raw_loaded = [sem(f"raw_loaded{ex}") for ex in range(E_)]
            sb3, psum3 = allocators(c2)
            ffn, ffn_credits = ffn_phase(sb3, psum3, sem, held, X, ident, ffn_w(WH), ffn_w(WL), small["ws"],
                                     small["bs"], small["iota"], sel8)
        with ExitStack() as c4:
            sb4, psum4 = allocators(c4)
            probs = sb4("probs", [P, 4, T])
            aw = {"probs": probs, "rel": probs[:, 0, :], "mask": probs[:, 1, :],
                  "raw_qk": probs[:, 2:4, :].rearrange("p a (g m) -> p a g m", g=GROUPS),
                  "qkh": sb4("w_qk_hi", [P, 2, GROUPS, P], F32R),
                  "qkl": sb4("w_qk_lo", [P, 2, GROUPS, P], F32R), "raw_v": sb4("w_v", [P, D]),
                  "vh": sb4("w_v_hi", [P, D], F32R), "vl": sb4("w_v_lo", [P, D], F32R),
                  "wp": sb4("w_proj", [P, GROUPS, D]), "bp": sb4("b_proj", [P, D]), "bv": sb4("b_v", [P, D]),
                  "bq": sb4("b_q", [P, GROUPS]), "bk": sb4("b_k", [P, GROUPS]), "bqs": sb4("b_q_scaled", [P, GROUPS]),
                  "slopes": sb4("slopes", [P, HEADS]),
                  "minus_lo": sb4("minus_lo", [P, 2])}
            att_loads = [(aw["raw_qk"], wqk), (aw["raw_v"][:], wv), (aw["wp"][:], wp), (aw["bp"][:], row(bp)),
                         (aw["bv"][:], row(bv)), (aw["bq"][:], bqk[:, 0, :]), (aw["bk"][:], bqk[:, 1, :]),
                         (aw["slopes"][:], row(slopes)), (aw["rel"], rel), (aw["mask"], mask),
                         (aw["minus_lo"][:], minus_lo)]
            att = attention_phase(sb4, psum4, sem, held, X, ident, aw)
        att_loaded = sem("att_loaded")
        split_hi, split_lo, ffn_ready, att_split = (sem(n) for n in ("split_hi", "split_lo", "ffn_ready", "att_split"))
        block = ctx.enter_context(nc.Block())

        @block.sync
        def _(sp):
            for dst, src in loads:
                sp.dma_start(dst, src).then_inc(loaded, 16)
            sp.wait_ge(phase_end, 4)
            for ex in range(E_):
                sp.dma_start(raw[:, ex, :], wffn[:, ex, :]).then_inc(raw_loaded[ex], 16)
            sp.wait_ge(phase_end, 8)
            for dst, src in att_loads:
                sp.dma_start(dst, src).then_inc(att_loaded, 16)
            sp.wait_ge(phase_end, 16)
            sp.dma_start(out.rearrange("b (s p) d -> p (b s) d", p=P),
                         X[:, 0:B * BLK].rearrange("p (n d) -> p n d", d=D)).then_inc(stored, 16)
            sp.wait_ge(stored, 16)

        def split_weights(e, which, n):
            if which == "act":
                for ex in {-1: (0, 1, 2), 0: (3, 4, 5), 1: (6, 7)}.get(n, ()):
                    e.wait_ge(raw_loaded[ex], 16)
                    e.activation(WH[:, ex, :], raw[:, ex, :], ACT.Copy).then_inc(split_hi, 1)
            if which == "dve":
                for ex in {0: (0, 1), 1: (2, 3), 3: (4, 5), 4: (6, 7)}.get(n, ()):
                    e.wait_ge(split_hi, ex + 1)
                    e.tensor_tensor(WL[:, ex, :], raw[:, ex, :], f32(WH[:, ex, :]), ALU.subtract)\
                        .then_inc(split_lo, 1)
            if which == "pe" and n == 2:
                e.wait_ge(split_lo, E_)
                e.wait_ge(ffn_ready, 3)

        def attention_weights(e, which):
            e.wait_ge(att_loaded, 16 * len(att_loads))
            if which == "act":
                e.activation(aw["qkh"][:], aw["raw_qk"], ACT.Copy).then_inc(att_split, 1)
                e.activation(aw["vh"][:], aw["raw_v"][:], ACT.Copy).then_inc(att_split, 1)
            if which == "dve":
                e.wait_ge(att_split, 2)
                e.tensor_tensor(aw["qkl"][:], aw["raw_qk"], f32(aw["qkh"][:]), ALU.subtract).then_inc(att_split, 1)
                e.tensor_tensor(aw["vl"][:], aw["raw_v"][:], f32(aw["vh"][:]), ALU.subtract).then_inc(att_split, 1)
            e.wait_ge(att_split, 4)

        def phases(e, which):
            mamba(e, which)
            barrier(e, phase_end, 1)
            ffn_credits(e, which)
            if which == "dve":
                e.memset(f32(sel8[:]), 0.0).then_inc(ffn_ready, 1)
                e.wait_ge(ffn_ready, 1)
                for row in (0, 32):
                    e.tensor_copy(sel8[row:row + E_],
                                  ident[0:E_, 0:E_].rearrange("p (n o) -> p n o", o=1).to_broadcast([E_, E_, P]))\
                        .then_inc(ffn_ready, 1)
            ffn(e, which, 0, split_weights)
            barrier(e, phase_end, 2)
            att(e, which, attention_weights)
            barrier(e, phase_end, 3)
            ffn(e, which, 1)
            barrier(e, phase_end, 4)

        @block.tensor
        def _(pe):
            phases(pe, "pe")

        @block.scalar
        def _(act):
            phases(act, "act")

        @block.vector
        def _(dve):
            phases(dve, "dve")

        @block.gpsimd
        def _(pool):
            phases(pool, "pool")


def kernel(**inputs):
    import numpy as np
    import concourse.bacc as bacc
    from concourse.bass_utils import run_bass_kernel_spmd

    m = {k.removeprefix("L0_"): np.asarray(v) for k, v in inputs.items()}
    a = lambda n: m["attn_a_" + n]

    def halves(v):
        return v.reshape(L, H, P, -1).transpose(2, 0, 1, 3)

    x_proj = np.concatenate([a("x_proj_w")[:, R:], a("x_proj_w")[:, :R]], axis=1)
    kqv, bkqv = m["attn_b_W_kqv"], m["attn_b_b_kqv"]

    def stacked(v):
        v = v.reshape(v.shape[0], GROUPS, 4, 1, DH)
        return np.broadcast_to(v, (v.shape[0], GROUPS, 4, 4, DH)).reshape(v.shape[0], GROUPS, P)

    wd = np.zeros((E_, 3 * P, D), np.float32)
    wd[:, :F_] = m["ffn_Wd"]
    wffn = np.concatenate([m["ffn_Wg"].transpose(1, 0, 2), m["ffn_Wu"].transpose(1, 0, 2),
                           wd.reshape(E_, 3, P, D).transpose(2, 0, 1, 3).reshape(P, E_, 3 * D)], axis=2)
    wp = np.zeros((GROUPS, 4, 32, D), np.float32)
    wp[:, :, :DH] = m["attn_b_W_proj"].reshape(GROUPS, 4, DH, D)
    col, part = np.arange(T) - 3 * P, np.arange(P)[:, None]
    copy = np.arange(P) // DH % 4
    arrays = {
        "x": a("x"), "win": a("in_proj_w").transpose(2, 0, 1), "cw": halves(a("conv_w")),
        "cb": halves(a("conv_b"))[..., 0], "xp": x_proj.transpose(0, 2, 1).reshape(L, H, P, 40).transpose(2, 0, 1, 3),
        "dtw": a("dt_proj_w").transpose(2, 0, 1), "dtb": halves(a("dt_proj_b"))[..., 0], "alog": halves(a("A_log")),
        "dskip": halves(a("Dskip"))[..., 0],
        "wout": a("out_proj_w").transpose(0, 2, 1).reshape(L, H, P, D).transpose(2, 0, 1, 3),
        "lnw": a("ln_w"), "lnb": a("ln_b"),
        "wqk": np.stack([stacked(kqv[:, D:2 * D]), stacked(kqv[:, 0:D])], axis=1),
        "bqk": np.stack([stacked(bkqv[None, D:2 * D])[0], stacked(bkqv[None, 0:D])[0]]).transpose(2, 0, 1),
        "wv": kqv[:, 2 * D:], "bv": bkqv[2 * D:], "wp": wp.reshape(GROUPS, P, D).transpose(1, 0, 2),
        "bp": m["attn_b_b_proj"], "slopes": m["attn_b_slopes"],
        "ws": m["ffn_Ws"], "bs": m["ffn_bs"], "wffn": wffn,
        "ident": np.eye(P, dtype=np.float32),
        "rel": (col - part).astype(np.float32), "mask": np.where(col > part, np.float32(NEG), np.float32(0)),
        "minus_lo": -np.stack([copy % 2, copy // 2], axis=1).astype(np.float32),
        "iota": np.broadcast_to(np.arange(E_, dtype=np.float32), (P, E_)),
    }
    arrays = {k: np.ascontiguousarray(v) for k, v in arrays.items()}
    nc = bacc.Bacc("TRN2", target_bir_lowering=False, num_devices=1)
    args = [nc.dram_tensor("in_" + k, v.shape, F32, kind="ExternalInput").ap() for k, v in arrays.items()]
    args.append(nc.dram_tensor("out_x", (B, T, D), F32, kind="ExternalOutput").ap())
    build(nc, *args)
    r = run_bass_kernel_spmd(nc, [{"in_" + k: v for k, v in arrays.items()}], core_ids=[0])
    return r.results[0]["out_x"]
```
